# Optimizing a Trainium2 kernel written in Bass

```python
import numpy as np
import jax
import jax.numpy as jnp

def _softmax(x, axis=-1):
    return jax.nn.softmax(x, axis=axis)

def _gelu(x):
    return jax.nn.gelu(x, approximate=True)

def _silu(x):
    return jax.nn.silu(x)

def _sigmoid(x):
    return jax.nn.sigmoid(x)

def _layernorm(x, axis=-1, eps=1e-05):
    m = jnp.mean(x, axis=axis, keepdims=True)
    v = jnp.var(x, axis=axis, keepdims=True)
    return (x - m) / jnp.sqrt(v + eps)

def _scatter_add(tgt, idx, src, axis=0):
    return tgt.at[idx].add(src)

def _segment_sum(src, seg, n):
    return jax.ops.segment_sum(src, seg, n)
kernel_name = 'mk_gnn_preln_d1_gnn_r8_1a4c0d'

def setup_inputs(seed: int=0):
    np.random.seed(seed)
    _w = jnp.asarray

    def _rec_inputs():
        import jax
        import jax.numpy as jnp
        _gk = jax.random.key(seed)
        x = -0.0005121 + 1.001 * jax.random.normal(jax.random.fold_in(_gk, 1), (6250, 64), jnp.float32)
        _s = jax.random.randint(jax.random.fold_in(_gk, 2), (100000,), 0, 6250, jnp.int32)
        _d = jax.random.randint(jax.random.fold_in(_gk, 3), (100000,), 0, 6250, jnp.int32)
        _loop = jnp.arange(6250, dtype=jnp.int32)
        src = jnp.concatenate([_s, _d, _loop])
        dst = jnp.concatenate([_d, _s, _loop])
        _o = jnp.argsort(dst, stable=True)
        src = src[_o]
        dst = dst[_o]
        edge_attr_64 = -8.16379e-05 + 0.999858 * jax.random.normal(jax.random.fold_in(_gk, 12), (206250, 64), jnp.float32)
        return (x, src, dst, edge_attr_64)
    x, src, dst, edge_attr_64 = _rec_inputs()

    def _L0_gnn_setup():
        import jax, jax.numpy as jnp
        import numpy as np
        N_NODES = 6250
        N_EDGES = 200000
        HID = 64
        key = jax.random.key(seed)
        ks = jax.random.split(key, 8)
        node_feat = jax.random.normal(ks[0], (N_NODES, HID), dtype=jnp.float32)
        edge_feat = jax.random.normal(ks[1], (N_EDGES, HID), dtype=jnp.float32)
        src = jax.random.randint(ks[2], (N_EDGES,), 0, N_NODES, dtype=jnp.int32)
        dst = jax.random.randint(ks[3], (N_EDGES,), 0, N_NODES, dtype=jnp.int32)
        s1 = 1.0 / np.sqrt(HID)
        s2 = 1.0 / np.sqrt(2 * HID)
        W1 = jax.random.uniform(ks[4], (HID, 2 * HID), jnp.float32, -s1, s1)
        b1 = jax.random.uniform(ks[5], (2 * HID,), jnp.float32, -s1, s1)
        W2 = jax.random.uniform(ks[6], (2 * HID, HID), jnp.float32, -s2, s2)
        b2 = jax.random.uniform(ks[7], (HID,), jnp.float32, -s2, s2)
        return {'node_feat': node_feat, 'edge_feat': edge_feat, 'src': src, 'dst': dst, 'W1': W1, 'b1': b1, 'W2': W2, 'b2': b2}
    _L0_gnn_all = _L0_gnn_setup()
    _L0_gnn_in = {k: v for k, v in _L0_gnn_all.items() if k in ('W1', 'b1', 'W2', 'b2')}
    del _L0_gnn_all
    return {'x': x, 'src': src, 'dst': dst, 'edge_attr_64': edge_attr_64, 'L0_gnn_W1': _L0_gnn_in['W1'], 'L0_gnn_b1': _L0_gnn_in['b1'], 'L0_gnn_W2': _L0_gnn_in['W2'], 'L0_gnn_b2': _L0_gnn_in['b2']}

def reference(x, src, dst, edge_attr_64, L0_gnn_W1, L0_gnn_b1, L0_gnn_W2, L0_gnn_b2):
    import jax
    import jax.numpy as jnp

    def _L0_gnn_ref(node_feat, edge_feat, src, dst, W1, b1, W2, b2):
        import jax, jax.numpy as jnp
        import numpy as np
        N_NODES = 6250
        N_EDGES = 200000
        HID = 64
        msg = node_feat[src] + edge_feat
        agg = jax.ops.segment_sum(msg, dst, num_segments=node_feat.shape[0])
        h = jax.nn.relu(agg @ W1 + b1)
        return h @ W2 + b2
    h = jnp.maximum(_layernorm(x, axis=-1), 0.0)
    x = x + _L0_gnn_ref(h, edge_attr_64, src, dst, L0_gnn_W1, L0_gnn_b1, L0_gnn_W2, L0_gnn_b2)
    return x

_drawn_inputs = setup_inputs


def setup_inputs(seed=0):
    import zlib

    import numpy as np

    out = dict(_drawn_inputs(seed))
    spreads = {}
    factors = {'L0_gnn_b1': 7.07, 'L0_gnn_b2': 3.761}
    for name, (base, spread) in spreads.items():
        noise = np.random.default_rng([zlib.crc32(name.encode()), seed]).standard_normal(out[name].shape)
        drawn = base * np.exp(spread * noise) if base else spread * noise
        out[name] = jnp.asarray(drawn.astype(out[name].dtype))
    for name, factor in factors.items():
        out[name] = (out[name] * factor).astype(out[name].dtype)
    return out
```

```python
import numpy as np
import concourse.bass as bass
from concourse import mybir
from contextlib import ExitStack


def build_gnn_layer(nc, x, src, dst, edge, w1, b1, w2, b2, out):
    f32, i32 = mybir.dt.float32, mybir.dt.int32
    ALU = mybir.AluOpType
    ACT = mybir.ActivationFunctionType
    AX = mybir.AxisListType

    P = 128
    N, F = x.shape
    E = dst.shape[0]
    HID = w1.shape[1]
    EPS = 1e-5
    FAR = 1.0e6

    K = 4
    CHUNK = P * K
    WINDOW = 32
    FULL = E // CHUNK
    CHUNKS = FULL + 1
    TWICE = CHUNKS * CHUNK - E
    GROUP = 8
    TILES = GROUP * K
    GROUPS = [(c, min(GROUP, CHUNKS - c)) for c in range(0, CHUNKS, GROUP)]
    STEPS = (FULL // GROUP - 2) // 2
    TAIL = 2 * STEPS
    ROWSETS = [(g, min(P, FULL - g)) for g in range(0, FULL, P)] + [(FULL, 1)]

    NT = -(-N // P)
    NLAST = N - (NT - 1) * P
    WIDTH = max(N + WINDOW, NT * P)
    BLK = 512
    BLOCKS = [(b, min(BLK, N - b)) for b in range(0, N, BLK)]

    h_dram = nc.dram_tensor("h_rows", (N, F), f32, kind="Internal").ap()

    ctx = ExitStack()
    with ctx:
        def sb(name, shape, dt=f32):
            return ctx.enter_context(nc.sbuf_tensor(name, shape, dt))

        def ps(name, shape, dt=f32):
            return ctx.enter_context(nc.psum_tensor(name, shape, dt))

        def sem(name):
            return ctx.enter_context(nc.semaphore(name))

        x_sb = sb("x_sb", [P, NT, F])
        h_sb = sb("h_sb", [P, NT, F])
        sq_sb = sb("sq_sb", [P, NT, F])
        mean = sb("mean", [P, NT])
        var = sb("var", [P, NT])
        std = sb("std", [P, NT])
        rstd = sb("rstd", [P, NT])
        eps_col = sb("eps_col", [P, 1])
        w1_sb = sb("w1_sb", [F, HID])
        w2_sb = sb("w2_sb", [HID, F])
        b1_col = sb("b1_col", [HID, 1])
        b2_all = sb("b2_all", [P, F])
        ident = sb("ident", [P, P])
        ones = sb("ones", [P, P])
        iota_w = sb("iota_w", [P, WINDOW])
        iota_p = sb("iota_p", [P, P])
        dst_row = sb("dst_row", [P, 2, CHUNK], i32)
        src_row = sb("src_row", [P, 2, CHUNK], i32)
        dst_rowf = sb("dst_rowf", [P, 2, CHUNK])
        src_rowf = sb("src_rowf", [P, 2, CHUNK])
        outside = sb("outside", [P, len(ROWSETS), 2])
        first_dst = sb("first_dst", [P, 1])
        rel_col = sb("rel_col", [P, CHUNKS, K])
        src_col = sb("src_col", [P, CHUNKS, K], i32)
        base_row = sb("base_row", [1, CHUNKS], i32)
        msg = [sb(f"msg{b}", [P, 2, TILES, F]) for b in range(2)]
        idx = [sb(f"idx{b}", [P, TILES], i32) for b in range(2)]
        onehot = [sb(f"onehot{b}", [P, TILES, WINDOW]) for b in range(2)]
        agg = sb("agg", [F, WIDTH])
        worst = sb("worst", [P, 1])
        flag_f = sb("flag_f", [1, 1])
        flag_i = sb("flag_i", [1, 1], i32)
        g_dst = sb("g_dst", [P, 1], i32)
        g_src = sb("g_src", [P, 1], i32)
        g_rel = sb("g_rel", [P, 1])
        g_far = sb("g_far", [P, 1])
        g_hot = sb("g_hot", [P, P])
        g_msg = sb("g_msg", [P, 2, F])
        hid_sb = [sb(f"hid_sb{b}", [HID, BLK]) for b in range(2)]
        o_sb = sb("o_sb", [P, NT, F])

        tr_ps = [ps(f"tr_ps{b}", [P, 512]) for b in range(2)]
        sum_ps = [ps(f"sum_ps{b}", [P, 512]) for b in range(2)]
        hid_ps = [ps(f"hid_ps{b}", [P, 512]) for b in range(2)]
        out_ps = [ps(f"out_ps{b}", [P, 512]) for b in range(2)]

        x_in, x_zero = sem("x_in"), sem("x_zero")
        w_in, base_in = sem("w_in"), sem("base_in")
        rows_in = [sem("rows_in0"), sem("rows_in1")]
        rows_used = sem("rows_used")
        const_made = sem("const_made")
        mean_sub, squared, var_made, std_made = sem("mean_sub"), sem("squared"), sem("var_made"), sem("std_made")
        h_made, h_out = sem("h_made"), sem("h_out")
        rows_float, turned, turned_used = sem("rows_float"), sem("turned"), sem("turned_used")
        edges_in = [sem("edges_in0"), sem("edges_in1")]
        gathered = [sem("gathered0"), sem("gathered1")]
        idx_made, hot_made = sem("idx_made"), sem("hot_made")
        summed, sums_added = sem("summed"), sem("sums_added")
        gather_turn = sem("gather_turn")
        dve_done = sem("dve_done")
        worst_made, worst_turned, flag_made = sem("worst_made"), sem("worst_turned"), sem("flag_made")

        def edge_rows(lo, chunks):
            return edge[bass.ds(lo, chunks * CHUNK), :].rearrange("(c p k) f -> p c (k f)", p=P, k=K)

        def slots(ap):
            return ap.rearrange("p (c k) f -> p c (k f)", k=K)

        def row_set(ap, lo, rows):
            return ap[lo:lo + rows * CHUNK].rearrange("(r e) -> r e", e=CHUNK)

        def col(ap, lo):
            return ap[bass.ds(lo, P)].rearrange("(p o) -> p o", o=1)

        def x_tiles(ap):
            return ap[0:(NT - 1) * P, :].rearrange("(t p) f -> p t f", p=P)

        with nc.Block() as block:

            @block.sync
            def _(sp):
                sp.wait_ge(x_zero, 1)
                sp.dma_start(x_sb[:, 0:NT - 1, :], x_tiles(x)).then_inc(x_in, 16)
                sp.dma_start(x_sb[0:NLAST, NT - 1, :], x[(NT - 1) * P:N, :]).then_inc(x_in, 16)
                for n, (first, rows) in enumerate(ROWSETS):
                    lo = min(first * CHUNK, E - CHUNK)
                    if n >= 2:
                        sp.wait_ge(rows_used, n - 1)
                    sp.dma_start(dst_row[0:rows, n % 2, :], row_set(dst, lo, rows)).then_inc(rows_in[n % 2], 16)
                    sp.dma_start(src_row[0:rows, n % 2, :], row_set(src, lo, rows)).then_inc(rows_in[n % 2], 16)

                def load_group(b, first, count):
                    on_grid = min(count, FULL - first)
                    if on_grid:
                        sp.dma_start(slots(msg[b][:, 0, 0:on_grid * K, :]),
                                     edge_rows(first * CHUNK, on_grid)).then_inc(edges_in[b], 16)
                    if on_grid < count:
                        sp.dma_start(slots(msg[b][:, 0, on_grid * K:count * K, :]),
                                     edge_rows(E - CHUNK, 1)).then_inc(edges_in[b], 16)

                for b in range(2):
                    load_group(b, b * GROUP, GROUP)
                with sp.Fori(1, STEPS) as i:
                    for b in range(2):
                        sp.wait_ge(summed, i * 2 + (b - 1))
                        sp.dma_start(slots(msg[b][:, 0, :, :]),
                                     edge_rows((i * 2 + b) * (GROUP * CHUNK), GROUP)).then_inc(edges_in[b], 16)
                for g in range(TAIL, len(GROUPS)):
                    sp.wait_ge(summed, g - 1)
                    load_group(g % 2, *GROUPS[g])

            @block.scalar
            def _(act):
                act.dma_start(w1_sb[:, :], w1[:, :]).then_inc(w_in, 16)
                act.dma_start(w2_sb[:, :], w2[:, :]).then_inc(w_in, 16)
                act.dma_start(b1_col[:, :], b1[:].rearrange("(p o) -> p o", o=1)).then_inc(w_in, 16)
                act.dma_start(b2_all[:, :], b2[:].rearrange("(o f) -> o f", o=1).to_broadcast([P, F])).then_inc(w_in, 16)
                with nc.allow_non_contiguous_dma(reason="one dst of each chunk"):
                    act.dma_start(base_row[0:1, 0:FULL],
                                  row_set(dst, 0, FULL)[:, 0:1].rearrange("r o -> o r")).then_inc(base_in, 16)
                act.dma_start(base_row[0:1, FULL:CHUNKS],
                              dst[E - CHUNK:E - CHUNK + 1].rearrange("(o r) -> o r", o=1)).then_inc(base_in, 16)
                act.wait_ge(mean_sub, 1)
                nc.scalar.activation(sq_sb[:, :, :], h_sb[:, :, :], ACT.Square).then_inc(squared, 1)
                act.wait_ge(var_made, 1)
                nc.scalar.activation(std[:, :], var[:, :], ACT.Sqrt, bias=eps_col[:, 0:1],
                                     scale=1.0 / F).then_inc(std_made, 1)
                act.wait_ge(h_made, 1)
                act.dma_start(x_tiles(h_dram), h_sb[:, 0:NT - 1, :]).then_inc(h_out, 16)
                act.dma_start(h_dram[(NT - 1) * P:N, :], h_sb[0:NLAST, NT - 1, :]).then_inc(h_out, 16)
                act.wait_ge(h_out, 32)

            @block.gpsimd
            def _(pool):
                nc.gpsimd.memset(ones[:, :], 1.0).then_inc(const_made, 1)
                nc.gpsimd.iota(iota_w[:, :], [[1, WINDOW]], base=0, channel_multiplier=0,
                               allow_small_or_imprecise_dtypes=True).then_inc(const_made, 1)
                nc.gpsimd.iota(iota_p[:, :], [[1, P]], base=0, channel_multiplier=0,
                               allow_small_or_imprecise_dtypes=True).then_inc(const_made, 1)
                pool.wait_ge(const_made, 3)
                nc.gpsimd.affine_select(out=ident[:, :], in_=ones[:, :], compare_op=ALU.is_equal, fill=0.0, base=0,
                                        pattern=[[-1, P]], channel_multiplier=1).then_inc(const_made, 1)

                def gather_group(b, tiles):
                    for t in range(tiles):
                        nc.gpsimd.indirect_dma_start(
                            out=msg[b][:, 1, t, :], out_offset=None, in_=h_dram[:, :],
                            in_offset=bass.IndirectOffsetOnAxis(ap=idx[b][:, t:t + 1], axis=0)).then_inc(gathered[b], 16)

                pool.wait_ge(h_out, 32)
                for b in range(2):
                    pool.wait_ge(idx_made, b + 1)
                    gather_group(b, TILES)
                with pool.Fori(1, STEPS) as i:
                    for b in range(2):
                        pool.wait_ge(idx_made, i * 2 + (b + 1))
                        pool.wait_ge(summed, i * 2 + (b - 1))
                        pool.sem_inc(gather_turn, 1)
                        gather_group(b, TILES)
                for g in range(TAIL, len(GROUPS)):
                    pool.wait_ge(idx_made, g + 1)
                    pool.wait_ge(summed, g - 1)
                    gather_group(g % 2, GROUPS[g][1] * K)

            @block.vector
            def _(dve):
                steps = [0]

                def chain(instruction):
                    steps[0] += 1
                    instruction.then_inc(dve_done, 1)
                    dve.wait_ge(dve_done, steps[0])

                nc.vector.memset(x_sb[:, NT - 1, :], 0.0).then_inc(x_zero, 1)
                nc.vector.memset(eps_col[:, :], EPS)
                nc.vector.memset(outside[:, :, :], 0.0)
                nc.vector.memset(agg[:, :], 0.0).then_inc(sums_added, 1)
                dve.wait_ge(sums_added, 1)

                def per_node(ap):
                    return ap[:, :].rearrange("p (t o) -> p t o", o=1).to_broadcast([P, NT, F])

                dve.wait_ge(x_in, 32)
                chain(nc.vector.tensor_reduce(mean[:, :], x_sb[:, :, :], AX.X, ALU.add))
                chain(nc.vector.tensor_scalar(mean[:, :], mean[:, :], 1.0 / F, None, ALU.mult))
                nc.vector.tensor_tensor(h_sb[:, :, :], x_sb[:, :, :], per_node(mean), ALU.subtract).then_inc(mean_sub, 1)
                dve.wait_ge(squared, 1)
                nc.vector.tensor_reduce(var[:, :], sq_sb[:, :, :], AX.X, ALU.add).then_inc(var_made, 1)
                dve.wait_ge(std_made, 1)
                chain(nc.vector.reciprocal(rstd[:, :], std[:, :]))
                chain(nc.vector.tensor_tensor(h_sb[:, :, :], h_sb[:, :, :], per_node(rstd), ALU.mult))
                nc.vector.tensor_scalar(h_sb[:, :, :], h_sb[:, :, :], 0.0, None, ALU.max).then_inc(h_made, 1)

                for n, (first, rows) in enumerate(ROWSETS):
                    b = n % 2
                    rel = dst_rowf[0:rows, b, :]
                    dve.wait_ge(rows_in[b], 32 * (n // 2 + 1))
                    if n >= 2:
                        dve.wait_ge(turned, 2 * (n - 1))
                    nc.vector.tensor_copy(src_rowf[0:rows, b, :], src_row[0:rows, b, :])
                    nc.vector.tensor_copy(rel, dst_row[0:rows, b, :]).then_inc(rows_used, 1)
                    dve.wait_ge(rows_used, n + 1)
                    chain(nc.vector.tensor_copy(first_dst[0:rows, :], dst_rowf[0:rows, b, 0:1]))
                    last = first == FULL and TWICE > 0
                    relative = nc.vector.tensor_scalar(rel, rel, first_dst[0:rows, 0:1], None, ALU.subtract)
                    if last:
                        chain(relative)
                    else:
                        relative.then_inc(rows_float, 1)
                        dve.wait_ge(rows_float, n + 1)
                    nc.vector.tensor_reduce(outside[0:rows, n, 0:1], rel, AX.X, ALU.max)
                    chain(nc.vector.tensor_reduce(outside[0:rows, n, 1:2], rel, AX.X, ALU.min))
                    if last:
                        nc.vector.tensor_scalar(dst_rowf[0:1, b, 0:TWICE], dst_rowf[0:1, b, 0:TWICE], FAR, None,
                                                ALU.add).then_inc(rows_float, 1)
                    for turn, dest in enumerate((rel_col, src_col)):
                        dve.wait_ge(turned, 2 * n + turn + 1)
                        nc.vector.tensor_copy(
                            dest[:, first:first + rows, :].rearrange("p r k -> p k r"),
                            tr_ps[turn][:, 0:K * P].rearrange("p (k r) -> p k r", k=K)[:, :, 0:rows]
                        ).then_inc(turned_used, 1)

                nc.vector.tensor_scalar(outside[:, :, 0], outside[:, :, 0], float(1 - WINDOW), None, ALU.add)
                chain(nc.vector.tensor_scalar(outside[:, :, 1], outside[:, :, 1], -1.0, None, ALU.mult))
                nc.vector.tensor_reduce(worst[:, :], outside[:, :, :], AX.XY, ALU.max).then_inc(worst_made, 1)
                dve.wait_ge(worst_turned, 1)
                chain(nc.vector.tensor_reduce(flag_f[:, :], tr_ps[0][0:1, 0:P], AX.X, ALU.max))
                chain(nc.vector.tensor_scalar(flag_f[:, :], flag_f[:, :], 0.0, 1.0, ALU.max, ALU.min))
                nc.vector.tensor_copy(flag_i[:, :], flag_f[:, :]).then_inc(flag_made, 1)

                rel_flat = rel_col[:, :, :].rearrange("p c k -> p (c k)")
                src_flat = src_col[:, :, :].rearrange("p c k -> p (c k)")

                def prepare(b, at, tiles):
                    nc.vector.tensor_copy(idx[b][:, 0:tiles], src_flat[:, bass.ds(at, tiles)]).then_inc(idx_made, 1)
                    nc.vector.tensor_tensor(
                        onehot[b][:, 0:tiles, :],
                        iota_w[:, :].rearrange("p (o w) -> p o w", o=1).to_broadcast([P, tiles, WINDOW]),
                        rel_flat[:, bass.ds(at, tiles)].rearrange("p (t o) -> p t o", o=1)
                        .to_broadcast([P, tiles, WINDOW]),
                        ALU.is_equal).then_inc(hot_made, 1)

                def add_group(b, first, chunks):
                    _, bases = nc.values_load_multi_w_load_instructions(
                        base_row[0:1, bass.ds(first, chunks)], engines=[mybir.EngineType.DVE],
                        min_val=0, max_val=N - 1, skip_runtime_bounds_check_because="dst is a node number")
                    for c in range(chunks):
                        window = agg[:, bass.ds(bases[c], WINDOW)]
                        dve.wait_ge(sums_added, first + (c + 1))
                        nc.vector.tensor_tensor(window, window, sum_ps[b][0:F, c * WINDOW:(c + 1) * WINDOW],
                                                ALU.add).then_inc(sums_added, 1)

                dve.wait_ge(const_made, 4)
                dve.wait_ge(base_in, 32)
                dve.wait_ge(turned_used, 2 * len(ROWSETS))
                for b in range(2):
                    prepare(b, b * TILES, TILES)
                with dve.Fori(0, STEPS) as i:
                    for b in range(2):
                        dve.wait_ge(summed, i * 2 + (b + 1))
                        add_group(b, dve.snap((i * 2 + b) * GROUP), GROUP)
                        prepare(b, dve.snap((i * 2 + (b + 2)) * TILES), TILES)
                for g in range(TAIL, len(GROUPS)):
                    dve.wait_ge(summed, g + 1)
                    add_group(g % 2, *GROUPS[g])
                    if g + 2 < len(GROUPS):
                        prepare(g % 2, GROUPS[g + 2][0] * K, GROUPS[g + 2][1] * K)

            @block.tensor
            def _(pe):
                pe.wait_ge(const_made, 4)
                for n, (first, rows) in enumerate(ROWSETS):
                    pe.wait_ge(rows_float, n + 1)
                    for turn, source in enumerate((dst_rowf, src_rowf)):
                        if n >= 1:
                            pe.wait_ge(turned_used, 2 * (n - 1) + turn + 1)
                        for k in range(K):
                            last = nc.tensor.transpose(tr_ps[turn][:, k * P:k * P + rows],
                                                       source[0:rows, n % 2, k:CHUNK:K], ident[0:rows, 0:rows])
                        last.then_inc(turned, 1)
                pe.wait_ge(worst_made, 1)
                nc.tensor.transpose(tr_ps[0][0:1, 0:P], worst[:, 0:1], ident[:, :]).then_inc(worst_turned, 1)

                def products(b, chunks):
                    for c in range(chunks):
                        for k in range(K):
                            t = c * K + k
                            for part in range(2):
                                last = nc.tensor.matmul(sum_ps[b][0:F, c * WINDOW:(c + 1) * WINDOW],
                                                        msg[b][:, part, t, :], onehot[b][:, t, :],
                                                        start=(k == 0 and part == 0),
                                                        stop=(k == K - 1 and part == 1))
                    last.then_inc(summed, 1)

                with pe.Fori(0, STEPS) as i:
                    for b in range(2):
                        pe.wait_ge(hot_made, i * 2 + (b + 1))
                        pe.wait_ge(edges_in[b], i * 16 + 16)
                        pe.wait_ge(gathered[b], i * (16 * TILES) + 16 * TILES)
                        products(b, GROUP)
                loads, gathers = [16 * STEPS] * 2, [16 * TILES * STEPS] * 2
                for g in range(TAIL, len(GROUPS)):
                    first, chunks = GROUPS[g]
                    loads[g % 2] += 16 * ((first < FULL) + (first + chunks > FULL))
                    gathers[g % 2] += 16 * chunks * K
                    pe.wait_ge(hot_made, g + 1)
                    pe.wait_ge(edges_in[g % 2], loads[g % 2])
                    pe.wait_ge(gathered[g % 2], gathers[g % 2])
                    products(g % 2, chunks)

        anew = nc.values_load(flag_i[0:1, 0:1], min_val=0, max_val=1,
                              skip_runtime_bounds_check_because="made as 0 or 1")
        g_cleared, g_in, g_read, g_gath, g_hots, g_sums, g_adds, g_cols, g_idx = [
            sem(s) for s in ("g_cleared", "g_in", "g_read", "g_gathered", "g_hot_made", "g_summed", "g_added",
                             "g_col_made", "g_idx_used")]
        G_TILES = E // P
        G_TWICE = (G_TILES + 1) * P - E
        with nc.If(anew):
            with nc.Block() as block:

                @block.sync
                def _(sp):
                    def load(lo, n):
                        sp.wait_ge(g_adds, n * NT + 1)
                        sp.dma_start(g_dst[:, :], col(dst, lo)).then_inc(g_in, 16)
                        sp.dma_start(g_src[:, :], col(src, lo)).then_inc(g_in, 16)

                    with sp.Fori(0, G_TILES) as i:
                        load(i * P, i)
                    load(E - P, G_TILES)

                @block.scalar
                def _(act):
                    def load(lo, n):
                        act.wait_ge(g_adds, n * NT + 1)
                        act.dma_start(g_msg[:, 0, :], edge[bass.ds(lo, P), :]).then_inc(g_in, 16)

                    with act.Fori(0, G_TILES) as i:
                        load(i * P, i)
                    load(E - P, G_TILES)

                @block.gpsimd
                def _(pool):
                    def gather(n):
                        pool.wait_ge(g_in, n * 48 + 48)
                        pool.sem_inc(gather_turn, 1)
                        nc.gpsimd.indirect_dma_start(
                            out=g_msg[:, 1, :], out_offset=None, in_=h_dram[:, :],
                            in_offset=bass.IndirectOffsetOnAxis(ap=g_src[:, 0:1], axis=0)).then_inc(g_gath, 16)

                    with pool.Fori(0, G_TILES) as i:
                        gather(i)
                    gather(G_TILES)

                @block.vector
                def _(dve):
                    def tile(n):
                        dve.wait_ge(g_in, n * 48 + 48)
                        nc.vector.tensor_copy(g_rel[:, :], g_dst[:, :]).then_inc(g_cols, 1)

                    def windows(n):
                        with dve.Fori(0, NT) as w:
                            done = dve.snap(n * NT + w)
                            dve.wait_ge(g_cols, n * (NT + 1) + w + 1)
                            nc.vector.tensor_scalar(g_hot[:, :], iota_p[:, :], g_rel[:, 0:1], None,
                                                    ALU.is_equal).then_inc(g_hots, 1)
                            nc.vector.tensor_scalar(g_rel[:, :], g_rel[:, :], float(-P), None, ALU.add).then_inc(g_cols, 1)
                            dve.wait_ge(g_sums, done + 1)
                            part = agg[:, bass.ds(w * P, P)]
                            nc.vector.tensor_tensor(part, part, sum_ps[0][0:F, 0:P], ALU.add).then_inc(g_adds, 1)

                    nc.vector.memset(g_far[:, :], 0.0).then_inc(g_cleared, 1)
                    dve.wait_ge(g_cleared, 1)
                    nc.vector.memset(g_far[0:G_TWICE, :], FAR).then_inc(g_cleared, 1)
                    nc.vector.memset(agg[:, :], 0.0).then_inc(g_adds, 1)
                    dve.wait_ge(g_cleared, 2)
                    dve.wait_ge(g_adds, 1)
                    with dve.Fori(0, G_TILES) as i:
                        tile(i)
                        windows(i)
                    tile(G_TILES)
                    dve.wait_ge(g_cols, G_TILES * (NT + 1) + 1)
                    nc.vector.tensor_tensor(g_rel[:, :], g_rel[:, :], g_far[:, :], ALU.add).then_inc(g_read, 1)
                    dve.wait_ge(g_read, 1)
                    windows(G_TILES)

                @block.tensor
                def _(pe):
                    def tile(n):
                        with pe.Fori(0, NT) as w:
                            pe.wait_ge(g_gath, n * 16 + 16)
                            pe.wait_ge(g_hots, n * NT + w + 1)
                            nc.tensor.matmul(sum_ps[0][0:F, 0:P], g_msg[:, 0, :], g_hot[:, :], start=True, stop=False)
                            nc.tensor.matmul(sum_ps[0][0:F, 0:P], g_msg[:, 1, :], g_hot[:, :],
                                             start=False, stop=True).then_inc(g_sums, 1)

                    with pe.Fori(0, G_TILES) as i:
                        tile(i)
                    tile(G_TILES)

        hid_made, relu_made, rows_made, rows_added, bias_added, rows_out = [
            sem(s) for s in ("hid_made", "relu_made", "rows_made", "rows_added", "bias_added", "rows_out")]
        with nc.Block() as block:
            BT = BLK // P

            def tiles_of(n):
                lo, count = BLOCKS[n]
                return [(t, min(P, lo + count - t)) for t in range(lo, lo + count, P)]

            @block.tensor
            def _(pe):
                def hidden(n):
                    lo, count = BLOCKS[n]
                    if n >= 2:
                        pe.wait_ge(relu_made, n - 1)
                    nc.tensor.matmul(hid_ps[n % 2][:, 0:count], w1_sb[:, :], agg[:, lo:lo + count],
                                     start=True, stop=True).then_inc(hid_made, 1)

                pe.wait_ge(w_in, 64)
                hidden(0)
                for n in range(len(BLOCKS)):
                    if n + 1 < len(BLOCKS):
                        hidden(n + 1)
                    pe.wait_ge(relu_made, n + 1)
                    if n >= 2:
                        pe.wait_ge(rows_added, n - 1)
                    for j, (lo, count) in enumerate(tiles_of(n)):
                        last = nc.tensor.matmul(out_ps[n % 2][0:count, j * F:(j + 1) * F],
                                                hid_sb[n % 2][:, j * P:j * P + count], w2_sb[:, :],
                                                start=True, stop=True)
                    last.then_inc(rows_made, 1)

            @block.scalar
            def _(act):
                act.wait_ge(w_in, 64)
                for n, (lo, count) in enumerate(BLOCKS):
                    act.wait_ge(hid_made, n + 1)
                    if n >= 2:
                        act.wait_ge(rows_made, n - 1)
                    nc.scalar.activation(hid_sb[n % 2][:, 0:count], hid_ps[n % 2][:, 0:count], ACT.Relu,
                                         bias=b1_col[:, 0:1]).then_inc(relu_made, 1)

            @block.vector
            def _(dve):
                dve.wait_ge(w_in, 64)
                nc.vector.tensor_tensor(x_sb[:, :, :], x_sb[:, :, :],
                                        b2_all[:, :].rearrange("p (o f) -> p o f", o=1).to_broadcast([P, NT, F]),
                                        ALU.add).then_inc(bias_added, 1)
                dve.wait_ge(bias_added, 1)
                for n in range(len(BLOCKS)):
                    dve.wait_ge(rows_made, n + 1)
                    parts = tiles_of(n)
                    whole = sum(count == P for _, count in parts)
                    t0 = n * BT
                    if whole:
                        last = nc.vector.tensor_tensor(
                            o_sb[:, t0:t0 + whole, :],
                            out_ps[n % 2][:, 0:whole * F].rearrange("p (t f) -> p t f", f=F),
                            x_sb[:, t0:t0 + whole, :], ALU.add)
                    if whole < len(parts):
                        count = parts[whole][1]
                        last = nc.vector.tensor_tensor(o_sb[0:count, t0 + whole, :],
                                                       out_ps[n % 2][0:count, whole * F:(whole + 1) * F],
                                                       x_sb[0:count, t0 + whole, :], ALU.add)
                    last.then_inc(rows_added, 1)

            @block.sync
            def _(sp):
                sent = 0
                for n in range(len(BLOCKS)):
                    sp.wait_ge(rows_added, n + 1)
                    parts = tiles_of(n)
                    whole = sum(count == P for _, count in parts)
                    t0 = n * BT
                    if whole:
                        sp.dma_start(out[t0 * P:(t0 + whole) * P, :].rearrange("(t p) f -> p t f", p=P),
                                     o_sb[:, t0:t0 + whole, :]).then_inc(rows_out, 16)
                        sent += 16
                    if whole < len(parts):
                        lo, count = parts[whole]
                        sp.dma_start(out[lo:lo + count, :], o_sb[0:count, t0 + whole, :]).then_inc(rows_out, 16)
                        sent += 16
                sp.wait_ge(rows_out, sent)


def kernel(**inputs):
    import concourse.bacc as bacc
    from concourse.bass_utils import run_bass_kernel_spmd

    nc = bacc.Bacc("TRN2", target_bir_lowering=False, num_devices=1)
    names = ["x", "src", "dst", "edge_attr_64", "L0_gnn_W1", "L0_gnn_b1", "L0_gnn_W2", "L0_gnn_b2"]
    arrays, args = {}, []
    for name in names:
        a = np.ascontiguousarray(inputs[name])
        arrays[f"in_{name}"] = a
        args.append(nc.dram_tensor(f"in_{name}", a.shape, mybir.dt.from_np(a.dtype), kind="ExternalInput").ap())
    args.append(nc.dram_tensor("out_0", inputs["x"].shape, mybir.dt.float32, kind="ExternalOutput").ap())
    build_gnn_layer(nc, *args)
    return run_bass_kernel_spmd(nc, [arrays], core_ids=[0]).results[0]["out_0"]
```

```python
import numpy as np
import concourse.bass as bass
from concourse import mybir
from contextlib import ExitStack


def build_gnn_layer(nc, x, src, dst, edge, w1, b1, w2, b2, out):
    f32, i32, bf16, f16 = mybir.dt.float32, mybir.dt.int32, mybir.dt.bfloat16, mybir.dt.float16
    ALU = mybir.AluOpType
    ACT = mybir.ActivationFunctionType
    AX = mybir.AxisListType

    P = 128
    N, F = x.shape
    E = dst.shape[0]
    HID = w1.shape[1]
    EPS = 1e-5
    FAR = 1.0e6
    NT = -(-N // P)
    NLAST = N - (NT - 1) * P

    K = 4
    CHUNK = P * K
    WINDOW = 32
    SPAN = 8
    CODES = NT * SPAN
    FULL = E // CHUNK
    CHUNKS = FULL + 1
    TWICE = CHUNKS * CHUNK - E

    CG = 8
    CT = CG * K
    PAIRS = CT // 2
    GG = 5
    GT = GG * K
    GROUPS = FULL // (2 * (CG + GG)) * 2
    COUNTED = GROUPS * CG
    GATHERED = [(c, min(GG, CHUNKS - c)) for c in range(COUNTED, CHUNKS, GG)]
    ROWSETS = [(c, min(P, FULL - c), False) for c in range(COUNTED, FULL, P)]
    ROWSETS[1:1] = [(c, min(P, COUNTED - c), True) for c in range(0, COUNTED, P)]
    ROWSETS.append((FULL, 1, False))

    WIDTH = max(N + WINDOW, NT * P)
    BLK = 512
    BLOCKS = [(b, min(BLK, N - b)) for b in range(0, N, BLK)]

    h_dram = nc.dram_tensor("h_rows", (N, F), f32, kind="Internal").ap()

    ctx = ExitStack()
    with ctx:
        def sb(name, shape, dt=f32):
            return ctx.enter_context(nc.sbuf_tensor(name, shape, dt))

        def ps(name, shape, dt=f32):
            return ctx.enter_context(nc.psum_tensor(name, shape, dt))

        def sem(name):
            return ctx.enter_context(nc.semaphore(name))

        ROOM = max(NT * CT * SPAN, 2 * 12 * CHUNK)
        counts = [sb(f"counts{b}", [P, ROOM], bf16) for b in range(2)]
        arena = [counts[b][:, :].bitcast(f32) for b in range(2)]
        taken = [0, 0]

        def carve(b, words):
            taken[b] += words
            assert taken[b] <= ROOM // 2
            return arena[b][:, taken[b] - words:taken[b]]

        dst_raw = [carve(0, CHUNK).bitcast(i32) for _ in range(2)]
        src_raw = [carve(0, CHUNK).bitcast(i32) for _ in range(2)]
        dst_f = carve(0, CHUNK)
        hi_raw = carve(0, CHUNK).bitcast(i32)
        rows_a = [carve(0, CHUNK) for _ in range(2)]
        rows_b = [carve(0, CHUNK) for _ in range(2)]
        rows_c = [carve(0, CHUNK) for _ in range(2)]
        sq_sb = carve(1, NT * F).rearrange("p (t f) -> p t f", f=F)

        x_sb = sb("x_sb", [P, NT, F])
        h_sb = sb("h_sb", [P, NT, F])
        o_sb = h_sb
        h_parts = sb("h_parts", [P, NT, 3, F], bf16)
        mean = sb("mean", [P, NT])
        var = sb("var", [P, NT])
        std = sb("std", [P, NT])
        rstd = sb("rstd", [P, NT])
        eps_col = sb("eps_col", [P, 1])
        w1_sb = sb("w1_sb", [2 * F, HID])
        w2_sb = sb("w2_sb", [HID, F])
        b1_col = sb("b1_col", [HID, 1])
        b2_all = sb("b2_all", [P, F])
        ident = sb("ident", [P, P])
        ones = sb("ones", [P, P])
        iota_w = sb("iota_w", [P, WINDOW])
        iota_p = sb("iota_p", [P, P])
        iota_c = sb("iota_c", [P, CODES], f16)
        iota_b = sb("iota_b", [P, P], bf16)
        outside = sb("outside", [P, len(ROWSETS), 4])
        rel_col = sb("rel_col", [P, CHUNKS, K])
        src_col = sb("src_col", [P, CHUNKS - COUNTED, K], i32)
        count_col = sb("count_col", [P, 2, COUNTED * K + CT])
        group_col = [sb(f"group_col{b}", [P, 2, CT]) for b in range(2)]
        base_row = sb("base_row", [1, CHUNKS], i32)
        tile_row = sb("tile_row", [1, COUNTED * K], i32)
        edges = [sb(f"edges{b}", [P, CT, F]) for b in range(2)]
        msg = [sb(f"msg{b}", [P, GT, 2, F]) for b in range(2)]
        idx = [sb(f"idx{b}", [P, GT], i32) for b in range(2)]
        e_hot = [sb(f"e_hot{b}", [P, CT, WINDOW]) for b in range(2)]
        m_hot = [sb(f"m_hot{b}", [P, GT, WINDOW]) for b in range(2)]
        SLOTS = 4
        EDGE_AT, MSG_AT, PART_AT = 8, 16, 24
        assert EDGE_AT + CG <= SLOTS * 4 and MSG_AT + GG < PART_AT and PART_AT + CT <= PAIRS * 4
        code_hot = [sb(f"code_hot{b}", [P, 2, CODES], bf16) for b in range(SLOTS)]
        lo_hot = [sb(f"lo_hot{b}", [P, 2, P], bf16) for b in range(SLOTS)]
        agg = sb("agg", [2 * F, WIDTH])
        worst = sb("worst", [P, 1])
        flag_f = sb("flag_f", [1, 1])
        flag_i = sb("flag_i", [1, 1], i32)
        g_dst = sb("g_dst", [P, 1], i32)
        g_src = sb("g_src", [P, 1], i32)
        g_rel = sb("g_rel", [P, 1])
        g_far = sb("g_far", [P, 1])
        g_hot = sb("g_hot", [P, P])
        g_msg = sb("g_msg", [P, 2, F])
        hid_sb = [e_hot[b][:, :, :].rearrange("p t w -> p (t w)")[:, 0:BLK] for b in range(2)]

        count_ps = [ps(f"count_ps{b}", [P, 2, 512]) for b in range(2)]
        part_ps = [ps(f"part_ps{b}", [P, 512]) for b in range(2)]
        edge_ps = ps("edge_ps", [P, 512])
        msg_ps = ps("msg_ps", [P, 512])
        turn_ps = part_ps
        hid_ps = part_ps
        out_ps = [count_ps[b][:, 0, :] for b in range(2)]
        sum_ps = [edge_ps]

        x_in, x_zero = sem("x_in"), sem("x_zero")
        w_in, base_in = sem("w_in"), sem("base_in")
        rows_in = [sem("rows_in0"), sem("rows_in1")]
        rows_used = sem("rows_used")
        const_made = sem("const_made")
        mean_sub, squared, var_made, std_made = sem("mean_sub"), sem("squared"), sem("var_made"), sem("std_made")
        h_made, h_out = sem("h_made"), sem("h_out")
        part_made, rest_made = sem("part_made"), sem("rest_made")
        rows_ready, turned, turned_used = sem("rows_ready"), sem("turned"), sem("turned_used")
        edges_in = [sem("edges_in0"), sem("edges_in1")]
        msg_in = [sem("msg_in0"), sem("msg_in1")]
        gathered = [sem("gathered0"), sem("gathered1")]
        idx_made = sem("idx_made")
        hots_made, counted, copied = sem("hots_made"), sem("counted"), sem("copied")
        parts_done, edges_done, msgs_done = sem("parts_done"), sem("edges_done"), sem("msgs_done")
        sums_added = sem("sums_added")
        gather_turn = sem("gather_turn")
        dve_done = sem("dve_done")
        worst_made, worst_turned, flag_made = sem("worst_made"), sem("worst_turned"), sem("flag_made")

        iota_made, columns_taken = sem("iota_made"), sem("columns_taken")
        JOB_ENDS = [sum(3 if s[2] else 2 for s in ROWSETS[:n + 1]) for n in range(len(ROWSETS))]
        JOBS = JOB_ENDS[-1]
        added = GROUPS * (CG + GG) + (GROUPS - 2) * CT + 1
        ADDED_BEFORE = {GROUPS: added}
        added += 2 * CT
        for n in range(GROUPS, len(GATHERED) - 1):
            added += GATHERED[n][1]
            ADDED_BEFORE[n + 1] = added

        def edge_rows(lo, chunks):
            return edge[bass.ds(lo, chunks * CHUNK), :].rearrange("(c p k) f -> p c (k f)", p=P, k=K)

        def row_set(ap, lo, rows):
            return ap[lo:lo + rows * CHUNK].rearrange("(r e) -> r e", e=CHUNK)

        def col(ap, lo):
            return ap[bass.ds(lo, P)].rearrange("(p o) -> p o", o=1)

        def x_tiles(ap):
            return ap[0:(NT - 1) * P, :].rearrange("(t p) f -> p t f", p=P)

        def wait(engine, semaphore, value):
            if not isinstance(value, int) or value > 0:
                engine.wait_ge(semaphore, value)

        def all_groups(engine, group):
            for b in range(2):
                group(b, b)
            with engine.Fori(1, GROUPS // 2) as i:
                for b in range(2):
                    group(i * 2 + b, b)

        def share(number, first, last, turn):
            if not first <= turn <= last:
                return range(0)
            n, t = last - first + 1, turn - first
            return range(number * t // n, number * (t + 1) // n)

        with nc.Block() as block:

            @block.sync
            def _(sp):
                sp.wait_ge(x_zero, 1)
                sp.dma_start(x_sb[:, 0:NT - 1, :], x_tiles(x)).then_inc(x_in, 16)
                sp.dma_start(x_sb[0:NLAST, NT - 1, :], x[(NT - 1) * P:N, :]).then_inc(x_in, 16)
                for n, (first, rows, _) in enumerate(ROWSETS):
                    lo = min(first * CHUNK, E - CHUNK)
                    if n >= 2:
                        sp.wait_ge(rows_used, n - 1)
                    sp.dma_start(dst_raw[n % 2][0:rows, :], row_set(dst, lo, rows)).then_inc(rows_in[n % 2], 16)
                    sp.dma_start(src_raw[n % 2][0:rows, :], row_set(src, lo, rows)).then_inc(rows_in[n % 2], 16)

                def load_msg(b, lo, chunks):
                    for c in range(chunks):
                        sp.dma_start(msg[b][:, c * K:(c + 1) * K, 0, :],
                                     edge[bass.ds(lo + c * CHUNK, CHUNK), :].rearrange("(p k) f -> p k f", k=K)
                                     ).then_inc(msg_in[b], 16)

                def group(g, b):
                    wait(sp, edges_done, g - 1)
                    sp.dma_start(edges[b][:, :, :].rearrange("p (c k) f -> p c (k f)", k=K),
                                 edge_rows(g * (CG * CHUNK), CG)).then_inc(edges_in[b], 16)
                    wait(sp, msgs_done, g - 1)
                    load_msg(b, g * (GG * CHUNK) + COUNTED * CHUNK, GG)

                all_groups(sp, group)
                for n in range(GROUPS, len(GATHERED)):
                    first, count = GATHERED[n]
                    on_grid = min(count, FULL - first)
                    sp.wait_ge(msgs_done, n - 1)
                    load_msg(n % 2, first * CHUNK, on_grid)
                    if on_grid < count:
                        sp.dma_start(msg[n % 2][:, on_grid * K:count * K, 0, :],
                                     edge[E - CHUNK:E, :].rearrange("(p k) f -> p k f", k=K)
                                     ).then_inc(msg_in[n % 2], 16)

            @block.scalar
            def _(act):
                with nc.allow_non_contiguous_dma(reason="one dst of each chunk and each tile"):
                    act.dma_start(base_row[0:1, 0:FULL],
                                  row_set(dst, 0, FULL)[:, 0:1].rearrange("r o -> o r")).then_inc(base_in, 16)
                    act.dma_start(tile_row[0:1, :],
                                  dst[0:COUNTED * CHUNK].rearrange("(r e) -> r e", e=P)[:, 0:1].rearrange("r o -> o r")
                                  ).then_inc(base_in, 16)
                act.dma_start(base_row[0:1, FULL:CHUNKS],
                              dst[E - CHUNK:E - CHUNK + 1].rearrange("(o r) -> o r", o=1)).then_inc(base_in, 16)
                act.wait_ge(mean_sub, 1)
                nc.scalar.activation(sq_sb, h_sb[:, :, :], ACT.Square).then_inc(squared, 1)
                act.wait_ge(var_made, 1)
                nc.scalar.activation(std[:, :], var[:, :], ACT.Sqrt, bias=eps_col[:, 0:1],
                                     scale=1.0 / F).then_inc(std_made, 1)
                act.wait_ge(h_made, 1)
                act.dma_start(x_tiles(h_dram), h_sb[:, 0:NT - 1, :]).then_inc(h_out, 16)
                act.dma_start(h_dram[(NT - 1) * P:N, :], h_sb[0:NLAST, NT - 1, :]).then_inc(h_out, 16)
                nc.scalar.copy(h_parts[:, :, 0, :], h_sb[:, :, :]).then_inc(part_made, 1)
                for part in (1, 2):
                    act.wait_ge(rest_made, part)
                    nc.scalar.copy(h_parts[:, :, part, :], sq_sb).then_inc(part_made, 1)
                act.dma_start(w1_sb[0:F, :], w1[:, :]).then_inc(w_in, 16)
                act.dma_start(w1_sb[F:2 * F, :], w1[:, :]).then_inc(w_in, 16)
                act.dma_start(w2_sb[:, :], w2[:, :]).then_inc(w_in, 16)
                act.dma_start(b1_col[:, :], b1[:].rearrange("(p o) -> p o", o=1)).then_inc(w_in, 16)
                act.dma_start(b2_all[:, :], b2[:].rearrange("(o f) -> o f", o=1).to_broadcast([P, F])).then_inc(w_in, 16)

                act.wait_ge(turned_used, JOBS)
                act.wait_ge(h_out, 32)

                def group(g, b):
                    places = counts[b][:, 0:NT * CT * SPAN].rearrange("p (s t w) -> p t s w", s=NT, w=SPAN)
                    wait(act, parts_done, g - 1)
                    for u in range(PAIRS):
                        act.wait_ge(counted, g * PAIRS + (u + 1))
                        nc.scalar.copy(places[:, 2 * u:2 * u + 2, :, :],
                                       count_ps[u % 2][:, :, 0:CODES].rearrange("p t (s w) -> p t s w", w=SPAN)
                                       ).then_inc(copied, 1)

                all_groups(act, group)

            @block.gpsimd
            def _(pool):
                nc.gpsimd.memset(ones[:, :], 1.0).then_inc(const_made, 1)
                nc.gpsimd.iota(iota_w[:, :], [[1, WINDOW]], base=0, channel_multiplier=0,
                               allow_small_or_imprecise_dtypes=True).then_inc(const_made, 1)
                nc.gpsimd.iota(iota_p[:, :], [[1, P]], base=0, channel_multiplier=0,
                               allow_small_or_imprecise_dtypes=True).then_inc(const_made, 1)
                nc.gpsimd.iota(iota_c[:, :], [[1, CODES]], base=0, channel_multiplier=0,
                               allow_small_or_imprecise_dtypes=True).then_inc(const_made, 1)
                pool.wait_ge(const_made, 4)
                nc.gpsimd.affine_select(out=ident[:, :], in_=ones[:, :], compare_op=ALU.is_equal, fill=0.0, base=0,
                                        pattern=[[-1, P]], channel_multiplier=1).then_inc(const_made, 1)
                nc.gpsimd.memset(agg[:, :], 0.0).then_inc(sums_added, 1)

                def gather(b, tiles):
                    for t in range(tiles):
                        nc.gpsimd.indirect_dma_start(
                            out=msg[b][:, t, 1, :], out_offset=None, in_=h_dram[:, :],
                            in_offset=bass.IndirectOffsetOnAxis(ap=idx[b][:, t:t + 1], axis=0)).then_inc(gathered[b], 16)

                def group(g, b):
                    wait(pool, idx_made, g + 1)
                    wait(pool, msgs_done, g - 1)
                    if not isinstance(g, int):
                        pool.sem_inc(gather_turn, 1)
                    gather(b, GT)

                pool.wait_ge(h_out, 32)
                all_groups(pool, group)
                for n in range(GROUPS, len(GATHERED)):
                    pool.wait_ge(idx_made, n + 1)
                    pool.wait_ge(msgs_done, n - 1)
                    gather(n % 2, GATHERED[n][1] * K)

            @block.vector
            def _(dve):
                steps = [0]

                def chain(instruction):
                    steps[0] += 1
                    instruction.then_inc(dve_done, 1)
                    dve.wait_ge(dve_done, steps[0])

                nc.vector.memset(x_sb[:, NT - 1, :], 0.0).then_inc(x_zero, 1)
                nc.vector.memset(eps_col[:, :], EPS)
                chain(nc.vector.memset(outside[:, :, :], 0.0))

                def per_node(ap):
                    return ap[:, :].rearrange("p (t o) -> p t o", o=1).to_broadcast([P, NT, F])

                dve.wait_ge(x_in, 32)
                chain(nc.vector.tensor_reduce(mean[:, :], x_sb[:, :, :], AX.X, ALU.add))
                chain(nc.vector.tensor_scalar(mean[:, :], mean[:, :], 1.0 / F, None, ALU.mult))
                nc.vector.tensor_tensor(h_sb[:, :, :], x_sb[:, :, :], per_node(mean), ALU.subtract).then_inc(mean_sub, 1)
                dve.wait_ge(squared, 1)
                nc.vector.tensor_reduce(var[:, :], sq_sb, AX.X, ALU.add).then_inc(var_made, 1)
                dve.wait_ge(std_made, 1)
                chain(nc.vector.reciprocal(rstd[:, :], std[:, :]))
                chain(nc.vector.tensor_tensor(h_sb[:, :, :], h_sb[:, :, :], per_node(rstd), ALU.mult))
                nc.vector.tensor_scalar(h_sb[:, :, :], h_sb[:, :, :], 0.0, None, ALU.max).then_inc(h_made, 1)

                def rows_of(n):
                    first, rows, is_counted = ROWSETS[n]
                    b = n % 2
                    raw_d, raw_s, df = dst_raw[b][0:rows, :], src_raw[b][0:rows, :], dst_f[0:rows, :]
                    a, second, third = rows_a[b][0:rows, :], rows_b[b][0:rows, :], rows_c[b][0:rows, :]

                    def tiles(ap):
                        return ap.rearrange("r (k e) -> r k e", k=K)

                    dve.wait_ge(rows_in[b], 32 * (n // 2 + 1))
                    if n >= 2:
                        dve.wait_ge(turned, JOB_ENDS[n - 2])
                    nc.vector.tensor_copy(df, raw_d)
                    if is_counted:
                        nc.vector.tensor_scalar(hi_raw[0:rows, :], raw_s, P.bit_length() - 1, SPAN.bit_length() - 1,
                                                ALU.logical_shift_right, ALU.logical_shift_left)
                        chain(nc.vector.tensor_scalar(raw_s, raw_s, P - 1, None, ALU.bitwise_and))
                        chain(nc.vector.tensor_copy(third, raw_s))
                        chain(nc.vector.tensor_tensor(tiles(second), tiles(df),
                                                      tiles(df)[:, :, 0:1].to_broadcast([rows, K, P]), ALU.subtract))
                        nc.vector.tensor_reduce(outside[0:rows, n, 2:3], second, AX.X, ALU.max)
                        chain(nc.vector.tensor_reduce(outside[0:rows, n, 3:4], second, AX.X, ALU.min))
                        chain(nc.vector.tensor_tensor(second, second, hi_raw[0:rows, :], ALU.add))
                    else:
                        chain(nc.vector.tensor_copy(second, raw_s))
                    relative = nc.vector.tensor_scalar(a, df, df[:, 0:1], None, ALU.subtract)
                    relative.then_inc(rows_used, 1)
                    dve.wait_ge(rows_used, n + 1)
                    nc.vector.tensor_reduce(outside[0:rows, n, 0:1], a, AX.X, ALU.max)
                    lowest = nc.vector.tensor_reduce(outside[0:rows, n, 1:2], a, AX.X, ALU.min)
                    if first == FULL and TWICE:
                        chain(lowest)
                        nc.vector.tensor_scalar(rows_a[b][0:1, 0:TWICE], rows_a[b][0:1, 0:TWICE], FAR, None,
                                                ALU.add).then_inc(rows_ready, 1)
                    else:
                        lowest.then_inc(rows_ready, 1)

                def columns_of(n):
                    first, rows, is_counted = ROWSETS[n]
                    at = first if is_counted else first - COUNTED
                    dests = [rel_col[:, first:first + rows, :]] + (
                        [count_col[:, part, at * K:(at + rows) * K].rearrange("p (r k) -> p r k", k=K) for part in range(2)]
                        if is_counted else [src_col[:, at:at + rows, :]])
                    for j, dest in enumerate(dests, JOB_ENDS[n] - len(dests)):
                        dve.wait_ge(turned, j + 1)
                        nc.vector.tensor_copy(
                            dest.rearrange("p r k -> p k r"),
                            turn_ps[j % 2][:, 0:K * P].rearrange("p (k r) -> p k r", k=K)[:, :, 0:rows]
                        ).then_inc(turned_used, 1)

                for n in range(len(ROWSETS)):
                    rows_of(n)
                    if n:
                        columns_of(n - 1)
                columns_of(len(ROWSETS) - 1)

                dve.wait_ge(part_made, 1)
                nc.vector.tensor_tensor(sq_sb, h_sb[:, :, :], h_parts[:, :, 0, :], ALU.subtract).then_inc(rest_made, 1)
                dve.wait_ge(part_made, 2)
                nc.vector.tensor_tensor(sq_sb, sq_sb, h_parts[:, :, 1, :], ALU.subtract).then_inc(rest_made, 1)

                for column, least in ((0, 1 - WINDOW), (2, 1 - SPAN)):
                    nc.vector.tensor_scalar(outside[:, :, column], outside[:, :, column], float(least), None, ALU.add)
                    last = nc.vector.tensor_scalar(outside[:, :, column + 1], outside[:, :, column + 1], -1.0, None,
                                                   ALU.mult)
                chain(last)
                nc.vector.tensor_reduce(worst[:, :], outside[:, :, :], AX.XY, ALU.max).then_inc(worst_made, 1)
                dve.wait_ge(worst_turned, 1)
                chain(nc.vector.tensor_reduce(flag_f[:, :], msg_ps[0:1, 0:P], AX.X, ALU.max))
                chain(nc.vector.tensor_scalar(flag_f[:, :], flag_f[:, :], 0.0, 1.0, ALU.max, ALU.min))
                nc.vector.tensor_copy(flag_i[:, :], flag_f[:, :]).then_inc(flag_made, 1)

                rel_flat = rel_col[:, :, :].rearrange("p c k -> p (c k)")
                src_flat = src_col[:, :, :].rearrange("p c k -> p (c k)")

                def windows(out_ap, at, tiles):
                    return nc.vector.tensor_tensor(
                        out_ap, iota_w[:, :].rearrange("p (o w) -> p o w", o=1).to_broadcast([P, tiles, WINDOW]),
                        rel_flat[:, bass.ds(at, tiles)].rearrange("p (t o) -> p t o", o=1)
                        .to_broadcast([P, tiles, WINDOW]), ALU.is_equal)

                def prepare_gather(b, g, tiles):
                    windows(m_hot[b][:, 0:tiles, :], COUNTED * K + g * GT, tiles)
                    nc.vector.tensor_copy(idx[b][:, 0:tiles], src_flat[:, bass.ds(g * GT, tiles)]).then_inc(idx_made, 1)

                def take_columns(b, g):
                    nc.vector.tensor_copy(group_col[b][:, :, :], count_col[:, :, bass.ds(g * CT, CT)]
                                          ).then_inc(columns_taken, 1)

                def load_bases(row, first, count):
                    _, bases = nc.values_load_multi_w_load_instructions(
                        row[0:1, bass.ds(first, count)], engines=[mybir.EngineType.DVE],
                        min_val=0, max_val=N - 1, skip_runtime_bounds_check_because="dst is a node number")
                    return bases

                def add_window(base, sums, done):
                    half, width = sums.shape
                    window = agg[0:half, bass.ds(base, width)]
                    dve.wait_ge(sums_added, done)
                    nc.vector.tensor_tensor(window, window, sums, ALU.add).then_inc(sums_added, 1)

                def chunk_sums(bank, half, c):
                    return bank[0:half, c * WINDOW:(c + 1) * WINDOW]

                def tile_sums(b, t):
                    return part_ps[b][:, t * SPAN:(t + 1) * SPAN]

                def done_before(g):
                    if isinstance(g, int) and g < 2:
                        return 1
                    return g * (CG + GG + CT) - (2 * CT + CG + GG - 1)

                AT_ONCE = 16

                def group(g, b):
                    behind = 2 if not isinstance(g, int) else g
                    done = done_before(g)
                    wait(dve, edges_done, g - 1)
                    windows(e_hot[b][:, :, :], g * CT, CT)
                    dve.wait_ge(columns_taken, g + 1)
                    part_bases = None
                    for h in range(4 * PAIRS):
                        u, j, by_lo = h // 4, h // 2 % 2, h % 2
                        slot, t = u % SLOTS, h // 2
                        if h % 4 == 0:
                            wait(dve, counted, g * PAIRS + (u - SLOTS + 1))
                        if by_lo:
                            made = nc.vector.tensor_scalar(lo_hot[slot][:, j, :], iota_b[:, :],
                                                           group_col[b][:, 1, t:t + 1], None, ALU.is_equal)
                        else:
                            made = nc.vector.tensor_scalar(code_hot[slot][:, j, :], iota_c[:, :],
                                                           group_col[b][:, 0, t:t + 1], None, ALU.is_equal)
                        if h % 4 == 3:
                            made.then_inc(hots_made, 1)

                        if EDGE_AT <= h < EDGE_AT + CG and behind >= 1:
                            if h == EDGE_AT:
                                dve.wait_ge(edges_done, g)
                                edge_bases = load_bases(base_row, (g - 1) * CG, CG)
                            c = h - EDGE_AT
                            add_window(edge_bases[c], chunk_sums(edge_ps, F, c), done + c)
                        if MSG_AT <= h < MSG_AT + GG and behind >= 1:
                            if h == MSG_AT:
                                dve.wait_ge(msgs_done, g)
                                msg_bases = load_bases(base_row, (g - 1) * GG + COUNTED, GG)
                            c = h - MSG_AT
                            add_window(msg_bases[c], chunk_sums(msg_ps, 2 * F, c), done + CG + c)
                        if h == MSG_AT + GG:
                            prepare_gather(1 - b, g + 1, GT)
                        if h == 4 * PAIRS - 1:
                            take_columns(1 - b, g + 1)
                        if PART_AT <= h < PART_AT + CT and behind >= 2:
                            if h == PART_AT:
                                dve.wait_ge(parts_done, g - 1)
                            t = h - PART_AT
                            if t % AT_ONCE == 0:
                                part_bases = load_bases(tile_row, (g - 2) * CT + t, AT_ONCE)
                            add_window(part_bases[t % AT_ONCE], tile_sums(b, t), done + (CG + GG) + t)

                def late_sums(n, done, chunks):
                    dve.wait_ge(msgs_done, n + 1)
                    bases = load_bases(base_row, GATHERED[n][0], chunks)
                    for c in range(chunks):
                        add_window(bases[c], chunk_sums(msg_ps, 2 * F, c), done + c)

                dve.wait_ge(const_made, 5)
                nc.vector.tensor_copy(iota_b[:, :], iota_p[:, :]).then_inc(iota_made, 1)
                dve.wait_ge(iota_made, 1)
                dve.wait_ge(base_in, 48)
                dve.wait_ge(turned_used, JOBS)
                nc.vector.memset(count_col[:, :, COUNTED * K:], 0.0)
                prepare_gather(0, 0, GT)
                take_columns(0, 0)
                all_groups(dve, group)
                done = done_before(GROUPS)
                dve.wait_ge(edges_done, GROUPS)
                bases = load_bases(base_row, COUNTED - CG, CG)
                for c in range(CG):
                    add_window(bases[c], chunk_sums(edge_ps, F, c), done + c)
                late_sums(GROUPS - 1, done + CG, GG)
                done += CG + GG
                prepare_gather((GROUPS + 1) % 2, GROUPS + 1, GATHERED[GROUPS + 1][1] * K)
                for g in (GROUPS - 2, GROUPS - 1):
                    dve.wait_ge(parts_done, g + 1)
                    for t in range(CT):
                        if t % AT_ONCE == 0:
                            bases = load_bases(tile_row, g * CT + t, AT_ONCE)
                        add_window(bases[t % AT_ONCE], tile_sums(g % 2, t), done + t)
                    done += CT
                for n in range(GROUPS, len(GATHERED)):
                    late_sums(n, done, GATHERED[n][1])
                    done += GATHERED[n][1]
                    if n + 2 < len(GATHERED):
                        prepare_gather(n % 2, n + 2, GATHERED[n + 2][1] * K)

            @block.tensor
            def _(pe):
                pe.wait_ge(const_made, 5)
                j = 0
                for n, (first, rows, is_counted) in enumerate(ROWSETS):
                    pe.wait_ge(rows_ready, n + 1)
                    sources = [(rows_a, True)] + ([(rows_b, False), (rows_c, False)] if is_counted else [(rows_b, True)])
                    for source, strided in sources:
                        if j >= 2:
                            pe.wait_ge(turned_used, j - 1)
                        for k in range(K):
                            part = source[n % 2][0:rows, k:CHUNK:K] if strided \
                                else source[n % 2][0:rows, k * P:(k + 1) * P]
                            last = nc.tensor.transpose(turn_ps[j % 2][:, k * P:k * P + rows], part,
                                                       ident[0:rows, 0:rows])
                        last.then_inc(turned, 1)
                        j += 1
                pe.wait_ge(worst_made, 1)
                nc.tensor.transpose(msg_ps[0:1, 0:P], worst[:, 0:1], ident[:, :]).then_inc(worst_turned, 1)

                def counts_times_h(g, b, his):
                    stacked = counts[b][:, 0:NT * CT * SPAN].rearrange("p (s c) -> p s c", s=NT)
                    for s in his:
                        whole = h_parts[:, s, 0:2, :].rearrange("p a f -> p (a f)")
                        last = nc.tensor.matmul(part_ps[b][:, 0:CT * SPAN], whole, stacked[:, s, :],
                                                start=(s == 0), stop=(s == NT - 1), skip_group_check=True)
                        half = F * (s % 2)
                        last = nc.tensor.matmul(part_ps[b][half:half + F, 0:CT * SPAN], h_parts[:, s, 2, :],
                                                stacked[:, s, :], start=False, stop=(s == NT - 1),
                                                skip_group_check=True)
                        if s == NT - 1:
                            last.then_inc(parts_done, 1)

                def gathered_products(b, chunks):
                    for c in range(chunks):
                        for t in range(c * K, (c + 1) * K):
                            last = nc.tensor.matmul(msg_ps[:, c * WINDOW:(c + 1) * WINDOW],
                                                    msg[b][:, t, :, :].rearrange("p a f -> p (a f)"),
                                                    m_hot[b][:, t, :], start=(t % K == 0), stop=(t % K == K - 1))
                    last.then_inc(msgs_done, 1)

                def group(g, b):
                    known = isinstance(g, int)
                    for u in range(PAIRS):
                        pe.wait_ge(hots_made, g * PAIRS + (u + 1))
                        wait(pe, copied, g * PAIRS + (u - 1))
                        for j in range(2):
                            last = nc.tensor.matmul(count_ps[u % 2][:, j, 0:CODES], lo_hot[u % SLOTS][:, j, :],
                                                    code_hot[u % SLOTS][:, j, :], start=True, stop=True)
                        last.then_inc(counted, 1)
                        if u == SLOTS:
                            if known:
                                pe.wait_ge(edges_in[b], 16 * (g // 2 + 1))
                            else:
                                pe.wait_ge(edges_in[b], g * 8 + (16 - 8 * b))
                        for t in share(CT, SLOTS, PAIRS - 1, u):
                            last = nc.tensor.matmul(edge_ps[0:F, t // K * WINDOW:(t // K + 1) * WINDOW],
                                                    edges[b][:, t, :], e_hot[b][:, t, :],
                                                    start=(t % K == 0), stop=(t % K == K - 1))
                            if t == CT - 1:
                                last.then_inc(edges_done, 1)
                        if not (known and g == 0):
                            if u == 2:
                                pe.wait_ge(copied, g * PAIRS)
                            counts_times_h(g - 1, 1 - b, share(NT, 2, PAIRS - 1, u))
                    if known:
                        pe.wait_ge(msg_in[b], 16 * GG * (g // 2 + 1))
                        pe.wait_ge(gathered[b], 16 * GT * (g // 2 + 1))
                    else:
                        pe.wait_ge(msg_in[b], g * (8 * GG) + (16 - 8 * b) * GG)
                        pe.wait_ge(gathered[b], g * (8 * GT) + (16 - 8 * b) * GT)
                    gathered_products(b, GG)

                pe.wait_ge(part_made, 3)
                all_groups(pe, group)
                pe.wait_ge(copied, GROUPS * PAIRS)
                counts_times_h(GROUPS - 1, (GROUPS - 1) % 2, range(NT))
                chunks_in = [GROUPS // 2 * GG] * 2
                for n in range(GROUPS, len(GATHERED)):
                    chunks = GATHERED[n][1]
                    chunks_in[n % 2] += chunks
                    pe.wait_ge(msg_in[n % 2], 16 * chunks_in[n % 2])
                    pe.wait_ge(gathered[n % 2], 16 * K * chunks_in[n % 2])
                    pe.wait_ge(sums_added, ADDED_BEFORE[n])
                    gathered_products(n % 2, chunks)

        anew = nc.values_load(flag_i[0:1, 0:1], min_val=0, max_val=1,
                              skip_runtime_bounds_check_because="made as 0 or 1")
        g_cleared, g_in, g_read, g_gath, g_hots, g_sums, g_adds, g_cols, g_idx = [
            sem(s) for s in ("g_cleared", "g_in", "g_read", "g_gathered", "g_hot_made", "g_summed", "g_added",
                             "g_col_made", "g_idx_used")]
        G_TILES = E // P
        G_TWICE = (G_TILES + 1) * P - E
        with nc.If(anew):
            with nc.Block() as block:

                @block.sync
                def _(sp):
                    def load(lo, n):
                        sp.wait_ge(g_adds, n * NT + 1)
                        sp.dma_start(g_dst[:, :], col(dst, lo)).then_inc(g_in, 16)
                        sp.dma_start(g_src[:, :], col(src, lo)).then_inc(g_in, 16)

                    with sp.Fori(0, G_TILES) as i:
                        load(i * P, i)
                    load(E - P, G_TILES)

                @block.scalar
                def _(act):
                    def load(lo, n):
                        act.wait_ge(g_adds, n * NT + 1)
                        act.dma_start(g_msg[:, 0, :], edge[bass.ds(lo, P), :]).then_inc(g_in, 16)

                    with act.Fori(0, G_TILES) as i:
                        load(i * P, i)
                    load(E - P, G_TILES)

                @block.gpsimd
                def _(pool):
                    def gather(n):
                        pool.wait_ge(g_in, n * 48 + 48)
                        pool.sem_inc(gather_turn, 1)
                        nc.gpsimd.indirect_dma_start(
                            out=g_msg[:, 1, :], out_offset=None, in_=h_dram[:, :],
                            in_offset=bass.IndirectOffsetOnAxis(ap=g_src[:, 0:1], axis=0)).then_inc(g_gath, 16)

                    with pool.Fori(0, G_TILES) as i:
                        gather(i)
                    gather(G_TILES)

                @block.vector
                def _(dve):
                    def tile(n):
                        dve.wait_ge(g_in, n * 48 + 48)
                        nc.vector.tensor_copy(g_rel[:, :], g_dst[:, :]).then_inc(g_cols, 1)

                    def windows(n):
                        with dve.Fori(0, NT) as w:
                            done = dve.snap(n * NT + w)
                            dve.wait_ge(g_cols, n * (NT + 1) + w + 1)
                            nc.vector.tensor_scalar(g_hot[:, :], iota_p[:, :], g_rel[:, 0:1], None,
                                                    ALU.is_equal).then_inc(g_hots, 1)
                            nc.vector.tensor_scalar(g_rel[:, :], g_rel[:, :], float(-P), None, ALU.add).then_inc(g_cols, 1)
                            dve.wait_ge(g_sums, done + 1)
                            part = agg[0:F, bass.ds(w * P, P)]
                            nc.vector.tensor_tensor(part, part, sum_ps[0][0:F, 0:P], ALU.add).then_inc(g_adds, 1)

                    nc.vector.memset(g_far[:, :], 0.0).then_inc(g_cleared, 1)
                    dve.wait_ge(g_cleared, 1)
                    nc.vector.memset(g_far[0:G_TWICE, :], FAR).then_inc(g_cleared, 1)
                    nc.vector.memset(agg[:, :], 0.0).then_inc(g_adds, 1)
                    dve.wait_ge(g_cleared, 2)
                    dve.wait_ge(g_adds, 1)
                    with dve.Fori(0, G_TILES) as i:
                        tile(i)
                        windows(i)
                    tile(G_TILES)
                    dve.wait_ge(g_cols, G_TILES * (NT + 1) + 1)
                    nc.vector.tensor_tensor(g_rel[:, :], g_rel[:, :], g_far[:, :], ALU.add).then_inc(g_read, 1)
                    dve.wait_ge(g_read, 1)
                    windows(G_TILES)

                @block.tensor
                def _(pe):
                    def tile(n):
                        with pe.Fori(0, NT) as w:
                            pe.wait_ge(g_gath, n * 16 + 16)
                            pe.wait_ge(g_hots, n * NT + w + 1)
                            nc.tensor.matmul(sum_ps[0][0:F, 0:P], g_msg[:, 0, :], g_hot[:, :], start=True, stop=False)
                            nc.tensor.matmul(sum_ps[0][0:F, 0:P], g_msg[:, 1, :], g_hot[:, :],
                                             start=False, stop=True).then_inc(g_sums, 1)

                    with pe.Fori(0, G_TILES) as i:
                        tile(i)
                    tile(G_TILES)

        hid_made, relu_made, rows_made, rows_added, bias_added, rows_out = [
            sem(s) for s in ("hid_made", "relu_made", "rows_made", "rows_added", "bias_added", "rows_out")]
        with nc.Block() as block:
            BT = BLK // P

            def tiles_of(n):
                lo, count = BLOCKS[n]
                return [(t, min(P, lo + count - t)) for t in range(lo, lo + count, P)]

            @block.tensor
            def _(pe):
                def hidden(n):
                    lo, count = BLOCKS[n]
                    if n >= 2:
                        pe.wait_ge(relu_made, n - 1)
                    nc.tensor.matmul(hid_ps[n % 2][:, 0:count], w1_sb[:, :], agg[:, lo:lo + count],
                                     start=True, stop=True).then_inc(hid_made, 1)

                pe.wait_ge(w_in, 80)
                hidden(0)
                for n in range(len(BLOCKS)):
                    if n + 1 < len(BLOCKS):
                        hidden(n + 1)
                    pe.wait_ge(relu_made, n + 1)
                    if n >= 2:
                        pe.wait_ge(rows_added, n - 1)
                    for j, (lo, count) in enumerate(tiles_of(n)):
                        last = nc.tensor.matmul(out_ps[n % 2][0:count, j * F:(j + 1) * F],
                                                hid_sb[n % 2][:, j * P:j * P + count], w2_sb[:, :],
                                                start=True, stop=True)
                    last.then_inc(rows_made, 1)

            @block.scalar
            def _(act):
                act.wait_ge(w_in, 80)
                for n, (lo, count) in enumerate(BLOCKS):
                    act.wait_ge(hid_made, n + 1)
                    if n >= 2:
                        act.wait_ge(rows_made, n - 1)
                    nc.scalar.activation(hid_sb[n % 2][:, 0:count], hid_ps[n % 2][:, 0:count], ACT.Relu,
                                         bias=b1_col[:, 0:1]).then_inc(relu_made, 1)

            @block.vector
            def _(dve):
                dve.wait_ge(w_in, 80)
                nc.vector.tensor_tensor(x_sb[:, :, :], x_sb[:, :, :],
                                        b2_all[:, :].rearrange("p (o f) -> p o f", o=1).to_broadcast([P, NT, F]),
                                        ALU.add).then_inc(bias_added, 1)
                dve.wait_ge(bias_added, 1)
                for n in range(len(BLOCKS)):
                    dve.wait_ge(rows_made, n + 1)
                    parts = tiles_of(n)
                    whole = sum(count == P for _, count in parts)
                    t0 = n * BT
                    if whole:
                        last = nc.vector.tensor_tensor(
                            o_sb[:, t0:t0 + whole, :],
                            out_ps[n % 2][:, 0:whole * F].rearrange("p (t f) -> p t f", f=F),
                            x_sb[:, t0:t0 + whole, :], ALU.add)
                    if whole < len(parts):
                        count = parts[whole][1]
                        last = nc.vector.tensor_tensor(o_sb[0:count, t0 + whole, :],
                                                       out_ps[n % 2][0:count, whole * F:(whole + 1) * F],
                                                       x_sb[0:count, t0 + whole, :], ALU.add)
                    last.then_inc(rows_added, 1)

            @block.sync
            def _(sp):
                sent = 0
                for n in range(len(BLOCKS)):
                    sp.wait_ge(rows_added, n + 1)
                    parts = tiles_of(n)
                    whole = sum(count == P for _, count in parts)
                    t0 = n * BT
                    if whole:
                        sp.dma_start(out[t0 * P:(t0 + whole) * P, :].rearrange("(t p) f -> p t f", p=P),
                                     o_sb[:, t0:t0 + whole, :]).then_inc(rows_out, 16)
                        sent += 16
                    if whole < len(parts):
                        lo, count = parts[whole]
                        sp.dma_start(out[lo:lo + count, :], o_sb[0:count, t0 + whole, :]).then_inc(rows_out, 16)
                        sent += 16
                sp.wait_ge(rows_out, sent)


def kernel(**inputs):
    import concourse.bacc as bacc
    from concourse.bass_utils import run_bass_kernel_spmd

    nc = bacc.Bacc("TRN2", target_bir_lowering=False, num_devices=1)
    names = ["x", "src", "dst", "edge_attr_64", "L0_gnn_W1", "L0_gnn_b1", "L0_gnn_W2", "L0_gnn_b2"]
    arrays, args = {}, []
    for name in names:
        a = np.ascontiguousarray(inputs[name])
        arrays[f"in_{name}"] = a
        args.append(nc.dram_tensor(f"in_{name}", a.shape, mybir.dt.from_np(a.dtype), kind="ExternalInput").ap())
    args.append(nc.dram_tensor("out_0", inputs["x"].shape, mybir.dt.float32, kind="ExternalOutput").ap())
    build_gnn_layer(nc, *args)
    return run_bass_kernel_spmd(nc, [arrays], core_ids=[0]).results[0]["out_0"]
```

```python
import numpy as np
import concourse.bass as bass
from concourse import mybir
from contextlib import ExitStack


def build_gnn_layer(nc, x, src, dst, edge, w1, b1, w2, b2, out):
    f32, i32, bf16, f16 = mybir.dt.float32, mybir.dt.int32, mybir.dt.bfloat16, mybir.dt.float16
    ALU = mybir.AluOpType
    ACT = mybir.ActivationFunctionType
    AX = mybir.AxisListType

    P = 128
    N, F = x.shape
    E = dst.shape[0]
    HID = w1.shape[1]
    EPS = 1e-5
    FAR = 1.0e6
    NT = -(-N // P)
    NLAST = N - (NT - 1) * P

    K = 4
    CHUNK = P * K
    WINDOW = 32
    SPAN = 8
    CODES = NT * SPAN
    FULL = E // CHUNK
    CHUNKS = FULL + 1
    TWICE = CHUNKS * CHUNK - E

    QUAD = 4
    QSPAN = P
    QT = QUAD * K
    assert QT * SPAN == P

    CG = 8
    CT = CG * K
    PAIRS = CT // 2
    QG = CG // QUAD
    GGS = (5, 4)
    GG = max(GGS)
    GT = GG * K
    GROUPS = -(-CHUNKS * 5 // 63)
    COUNTED = GROUPS * CG
    QUADS = COUNTED // QUAD
    REST = CHUNKS - COUNTED
    LOOPED = max(l for l in range(0, GROUPS + 1, 2)
                 if l // 2 * sum(GGS) <= FULL - COUNTED and l // 2 * sum(GGS) + (GROUPS - l) * GG >= REST)
    GATHERED = [(COUNTED + g // 2 * sum(GGS) + g % 2 * GGS[0], GGS[g % 2]) for g in range(LOOPED)]
    GATHERED += [(c, min(GG, CHUNKS - c)) for c in range(COUNTED + LOOPED // 2 * sum(GGS), CHUNKS, GG)]
    assert LOOPED >= 4 and len(GATHERED) <= GROUPS
    ROWSETS = [(c, min(P, CHUNKS - c), False) for c in range(COUNTED, CHUNKS, P)]
    ROWSETS[1:1] = [(c, min(P, COUNTED - c), True) for c in range(0, COUNTED, P)]
    assert QUADS <= P and ROWSETS[0][1] >= 2 * GG and len(ROWSETS) <= 4 and ROWSETS[1][1] >= 3 * CG

    WIDTH = N + QSPAN
    BLK = 512
    BLOCKS = [(b, min(BLK, N - b)) for b in range(0, N, BLK)]

    h_dram = nc.dram_tensor("h_rows", (P * NT, F), f32, kind="Internal").ap()

    ctx = ExitStack()
    with ctx:
        def sb(name, shape, dt=f32):
            return ctx.enter_context(nc.sbuf_tensor(name, shape, dt))

        def ps(name, shape, dt=f32):
            return ctx.enter_context(nc.psum_tensor(name, shape, dt))

        def sem(name):
            return ctx.enter_context(nc.semaphore(name))

        LB = 8
        ROOM = max(NT * CT * SPAN, 2 * 12 * CHUNK)
        counts = [sb(f"counts{b}", [P, ROOM], bf16) for b in range(2)]
        arena = [counts[b][:, :].bitcast(f32) for b in range(2)]
        taken = [0, 0]

        def carve(b, words):
            taken[b] += words
            assert taken[b] <= ROOM // 2
            return arena[b][:, taken[b] - words:taken[b]]

        dst_raw = [carve(0, CHUNK).bitcast(i32) for _ in range(2)]
        src_raw = [carve(0, CHUNK).bitcast(i32) for _ in range(2)]
        dst_f = carve(0, CHUNK)
        hi_raw = carve(0, CHUNK).bitcast(i32)
        rows_a = [carve(0, CHUNK) for _ in range(2)]
        rows_b = [carve(0, CHUNK) for _ in range(2)]
        rows_c = [carve(0, CHUNK) for _ in range(2)]
        sq_sb = carve(1, NT * F).rearrange("p (t f) -> p t f", f=F)
        pool_rows = [carve(1, CHUNK) for _ in range(6)] if len(ROWSETS) > 2 else []

        x_sb = sb("x_sb", [P, NT, F])
        h_sb = sb("h_sb", [P, NT, F])
        o_sb = h_sb
        LATER = [x_sb[:, :, :].rearrange("p t f -> p (t f)")[:, k * CHUNK:(k + 1) * CHUNK] for k in range(6)] \
            if len(ROWSETS) > 3 else []
        assert not LATER or 6 * CHUNK <= NT * F
        h_parts = sb("h_parts", [P, NT, 3, F], bf16)
        mean = sb("mean", [P, NT])
        var = sb("var", [P, NT])
        std = sb("std", [P, NT])
        rstd = sb("rstd", [P, NT])
        eps_col = sb("eps_col", [P, 1])
        w1_sb = sb("w1_sb", [2 * F, HID])
        w2_sb = sb("w2_sb", [HID, F])
        b1_col = sb("b1_col", [HID, 1])
        b2_all = sb("b2_all", [P, F])
        ident = sb("ident", [P, P])
        ones = sb("ones", [P, P])
        iota_w = sb("iota_w", [P, WINDOW])
        iota_p = sb("iota_p", [P, P])
        iota_c = sb("iota_c", [P, CODES], f16)
        iota_b = sb("iota_b", [P, P, LB], bf16)
        outside = sb("outside", [P, len(ROWSETS) + 1, 4])
        rel_col = sb("rel_col", [P, CHUNKS + GG, K])
        src_col = sb("src_col", [P, CHUNKS - COUNTED, K], i32)
        count_col = sb("count_col", [P, 2, COUNTED * K + CT])
        place_col = sb("place_col", [P, QUADS])
        group_code = [sb(f"group_code{b}", [P, CT]) for b in range(2)]
        group_lo = [sb(f"group_lo{b}", [P, CT], bf16) for b in range(2)]
        quad_first = sb("quad_first", [QUADS, QT], i32)
        quad_rel = sb("quad_rel", [QUADS, QT])
        quad_rows = sb("quad_rows", [QUADS, QT, SPAN])
        base_row = sb("base_row", [1, CHUNKS], i32)
        quad_row = sb("quad_row", [1, QUADS], i32)
        edges = [sb(f"edges{b}", [P, CT, F]) for b in range(2)]
        msg = [sb(f"msg{b}", [P, GT, F]) for b in range(2)]
        idx = [sb(f"idx{b}", [P, GT], i32) for b in range(2)]
        e_hot = [sb(f"e_hot{b}", [P, CT, WINDOW]) for b in range(2)]
        m_hot = [sb(f"m_hot{b}", [P, GT, WINDOW]) for b in range(2)]
        parts_sb = sb("parts_sb", [P, QG, 3 * F])
        place_hot = sb("place_hot", [P, QG, QSPAN])
        SLOTS = 4
        EDGE_AT, MSG_AT, PLACE_AT = 8, 18, 23
        EDGE_FROM = (EDGE_AT + CG) // 2
        assert MSG_AT >= EDGE_AT + CG and PLACE_AT >= MSG_AT + GG and PLACE_AT + QG < CT and LB == 2 * SLOTS
        TURN_AT = {2: 2, 3: 8}
        QUADS_AT, WORST_AT = 11, 14
        code_hot = [sb(f"code_hot{b}", [P, 2, CODES], bf16) for b in range(SLOTS)]
        lo_hot = [sb(f"lo_hot{b}", [P, P, LB], bf16) for b in range(2)]
        agg = sb("agg", [2 * F, WIDTH])
        worst = sb("worst", [P, 1])
        flag_f = sb("flag_f", [1, 1])
        flag_i = sb("flag_i", [1, 1], i32)
        g_dst = sb("g_dst", [P, 1], i32)
        g_src = sb("g_src", [P, 1], i32)
        g_hi = sb("g_hi", [P, 1], i32)
        g_row = sb("g_row", [P, 1], i32)
        g_rel = sb("g_rel", [P, 1])
        g_far = sb("g_far", [P, 1])
        g_hot = sb("g_hot", [P, P])
        g_msg = sb("g_msg", [P, 2, F])
        hid_sb = [e_hot[b][:, :, :].rearrange("p t w -> p (t w)")[:, 0:BLK] for b in range(2)]

        count_ps = [ps(f"count_ps{b}", [P, 2, 512]) for b in range(2)]
        part_ps = ps("part_ps", [P, 512])
        placed_ps = ps("placed_ps", [P, 512])
        edge_ps = ps("edge_ps", [P, 512])
        msg_ps = ps("msg_ps", [P, 512])
        turn_ps = [part_ps, placed_ps]
        hid_ps = [part_ps, placed_ps]
        out_ps = [count_ps[b][:, 0, :] for b in range(2)]
        sum_ps = [edge_ps]

        SLICES = 4
        CUTS = [NT * s // SLICES for s in range(SLICES + 1)]
        x_again = sem("x_again")
        x_in, x_zero = [sem(f"x_in{s}") for s in range(SLICES)], sem("x_zero")
        w_in, base_in = sem("w_in"), sem("base_in")
        rows_in = [sem(f"rows_in{n}") for n in range(len(ROWSETS))]
        const_made = sem("const_made")
        mean_sub, squared, var_made, std_made = sem("mean_sub"), sem("squared"), sem("var_made"), sem("std_made")
        h_made, h_out = sem("h_made"), sem("h_out")
        part_made, rest_made = sem("part_made"), sem("rest_made")
        rows_ready = [sem(f"rows_ready{n}") for n in range(len(ROWSETS))]
        rows_measured, outside_cleared, quads_ready = sem("rows_measured"), sem("outside_cleared"), sem("quads_ready")
        pool_done, src_split = sem("pool_done"), sem("src_split")
        turned, turned_used = sem("turned"), sem("turned_used")
        edges_in = [sem("edges_in0"), sem("edges_in1")]
        msg_in = [sem("msg_in0"), sem("msg_in1")]
        gathered = [sem("gathered0"), sem("gathered1")]
        idx_made = sem("idx_made")
        hots_made, counted, copied = sem("hots_made"), sem("counted"), sem("copied")
        parts_done, edges_done, msgs_done = sem("parts_done"), sem("edges_done"), sem("msgs_done")
        parts_copied, place_made, placed = sem("parts_copied"), sem("place_made"), sem("placed")
        m_hots_made = sem("m_hots_made")
        sums_added = sem("sums_added")
        gather_turn = sem("gather_turn")
        dve_done = sem("dve_done")
        worst_made, worst_turned, flag_made = sem("worst_made"), sem("worst_turned"), sem("flag_made")
        bias_added = sem("bias_added")
        iota_made, columns_taken = sem("iota_made"), sem("columns_taken")
        JOB_ENDS = [sum(3 if s[2] else 2 for s in ROWSETS[:n + 1]) for n in range(len(ROWSETS))]
        JOBS = JOB_ENDS[-1] + 1

        TURN_BANK = [j % 2 for j in range(JOBS - 1)] + [1]

        def turn_free(j):
            return max([i + 1 for i in range(j) if TURN_BANK[i] == TURN_BANK[j]], default=0)

        def gathered_chunks(g, b):
            if not isinstance(g, int):
                return GGS[b]
            return GATHERED[g][1] if 0 <= g < len(GATHERED) else 0

        def gathered_first(g, b, i):
            if isinstance(g, int):
                return GATHERED[g][0] - COUNTED
            return i * sum(GGS) + b * GGS[0]

        def done_before(g, b=0, i=0):
            if not isinstance(g, int):
                gathered_so_far = i * sum(GGS) - (GGS[1] if b == 0 else 0)
                return g * (CG + QG) + (gathered_so_far + (1 - CG - 2 * QG))
            return 1 + max(g - 1, 0) * CG + sum(gathered_chunks(n, n % 2) for n in range(g - 1)) + max(g - 2, 0) * QG

        msg_dmas = [min(1, FULL - first) + (first + count > FULL) for first, count in GATHERED]

        def edge_rows(lo, chunks):
            return edge[bass.ds(lo, chunks * CHUNK), :].rearrange("(c p k) f -> p c (k f)", p=P, k=K)

        def row_set(ap, lo, rows):
            return ap[lo:lo + rows * CHUNK].rearrange("(r e) -> r e", e=CHUNK)

        def col(ap, lo):
            return ap[bass.ds(lo, P)].rearrange("(p o) -> p o", o=1)

        def x_tiles(ap):
            return ap[0:(NT - 1) * P, :].rearrange("(t p) f -> p t f", p=P)

        def wait(engine, semaphore, value):
            if not isinstance(value, int) or value > 0:
                engine.wait_ge(semaphore, value)

        def all_groups(engine, group):
            for b in range(2):
                group(b, b, 0)
            with engine.Fori(1, LOOPED // 2) as i:
                for b in range(2):
                    group(i * 2 + b, b, i)
            for g in range(LOOPED, GROUPS):
                group(g, g % 2, g // 2)

        def share(number, first, last, turn):
            if not first <= turn <= last:
                return range(0)
            n, t = last - first + 1, turn - first
            return range(number * t // n, number * (t + 1) // n)

        with nc.Block() as block:

            def load_x(engine, s):
                lo, hi = CUTS[s], CUTS[s + 1]
                full = min(hi, NT - 1)
                if lo < full:
                    engine.dma_start(x_sb[:, lo:full, :], x_tiles(x)[:, lo:full, :]).then_inc(x_in[s], 16)
                if hi == NT:
                    engine.dma_start(x_sb[0:NLAST, NT - 1, :], x[(NT - 1) * P:N, :]).then_inc(x_in[s], 16)

            def row_buffers(n):
                rows = ROWSETS[n][1]
                if n < 2:
                    chosen = [dst_raw[n], src_raw[n], dst_f, hi_raw, rows_a[n], rows_b[n], rows_c[n]]
                else:
                    six = pool_rows if n == 2 else LATER
                    chosen = [six[0].bitcast(i32), six[1].bitcast(i32), six[2], six[3].bitcast(i32),
                              six[4], six[5], six[0]]
                return [buffer[0:rows, :] for buffer in chosen]

            def load_rows(engine, n):
                first, rows, _ = ROWSETS[n]
                raw_d, raw_s = row_buffers(n)[0:2]
                for ap, raw in ((dst, raw_d), (src, raw_s)):
                    on_grid = min(rows, FULL - first)
                    engine.dma_start(raw[0:on_grid, :], row_set(ap, first * CHUNK, on_grid)
                                     ).then_inc(rows_in[n], 16)
                    if on_grid < rows:
                        engine.dma_start(raw[on_grid:rows, :], row_set(ap, E - CHUNK, 1)
                                         ).then_inc(rows_in[n], 16)

            rows_dmas = [4 if first + rows == CHUNKS else 2 for first, rows, _ in ROWSETS]

            def split_src(n):
                raw_s, _, hi = row_buffers(n)[1:4]
                if ROWSETS[n][2]:
                    nc.vector.tensor_scalar(hi, raw_s, P.bit_length() - 1, SPAN.bit_length() - 1,
                                            ALU.logical_shift_right, ALU.logical_shift_left)
                else:
                    nc.vector.tensor_scalar(hi, raw_s, P.bit_length() - 1, None, ALU.logical_shift_right)
                return nc.vector.tensor_scalar(raw_s, raw_s, P - 1, None, ALU.bitwise_and)

            def rows_of(engine, vector, chain, n):
                rows, is_counted = ROWSETS[n][1:]
                raw_d, raw_s, df, hi, a, second, third = row_buffers(n)

                def tiles(ap):
                    return ap.rearrange("r (k e) -> r k e", k=K)

                engine.wait_ge(rows_in[n], 16 * rows_dmas[n])
                chain(vector.tensor_copy(df, raw_d))
                if n == 2:
                    engine.wait_ge(src_split, 1)
                else:
                    chain(split_src(n))
                vector.tensor_scalar(a, df, df[:, 0:1], None, ALU.subtract)
                if is_counted:
                    if n == 2:
                        chain(vector.tensor_copy(third, raw_s))
                        vector.tensor_copy(raw_s.bitcast(f32), hi)
                        hi = raw_s.bitcast(f32)
                    else:
                        vector.tensor_copy(third, raw_s)
                    chain(vector.tensor_tensor(tiles(second), tiles(df),
                                               tiles(df)[:, :, 0:1].to_broadcast([rows, K, P]), ALU.subtract))
                    vector.tensor_tensor(df, second, hi, ALU.add).then_inc(rows_ready[n], 1)
                else:
                    vector.scalar_tensor_tensor(out=second, in0=raw_s, scalar=float(NT), in1=hi,
                                                op0=ALU.mult, op1=ALU.add).then_inc(rows_ready[n], 1)

            @block.sync
            def _(sp):
                load_rows(sp, 0)
                for s in range(0, SLICES, 2):
                    if CUTS[s + 1] == NT:
                        sp.wait_ge(x_zero, 1)
                    load_x(sp, s)
                if pool_rows:
                    load_rows(sp, 2)
                load_rows(sp, 1)
                for s in range(SLICES):
                    sp.wait_ge(h_made, s + 1)
                    sp.dma_start(h_dram.rearrange("(p t) f -> p t f", t=NT)[:, CUTS[s]:CUTS[s + 1], :],
                                 h_sb[:, CUTS[s]:CUTS[s + 1], :]).then_inc(h_out, 16)
                if LATER:
                    load_rows(sp, 3)

                def load_msg(b, lo, chunks):
                    sp.dma_start(msg[b][:, 0:chunks * K, :].rearrange("p (c k) f -> p c (k f)", k=K),
                                 edge_rows(lo, chunks)).then_inc(msg_in[b], 16)

                def load_known_msg(n):
                    first, count = GATHERED[n]
                    on_grid = min(count, FULL - first)
                    if on_grid:
                        load_msg(n % 2, first * CHUNK, on_grid)
                    if on_grid < count:
                        sp.dma_start(msg[n % 2][:, on_grid * K:count * K, :],
                                     edge[E - CHUNK:E, :].rearrange("(p k) f -> p k f", k=K)
                                     ).then_inc(msg_in[n % 2], 16)

                def group(g, b, i):
                    wait(sp, edges_done, g - 1)
                    sp.dma_start(edges[b][:, :, :].rearrange("p (c k) f -> p c (k f)", k=K),
                                 edge_rows(g * (CG * CHUNK), CG)).then_inc(edges_in[b], 16)
                    if not gathered_chunks(g, b):
                        return
                    wait(sp, msgs_done, g - 1)
                    if isinstance(g, int):
                        load_known_msg(g)
                    else:
                        load_msg(b, gathered_first(g, b, i) * CHUNK + COUNTED * CHUNK, GGS[b])

                all_groups(sp, group)

            @block.scalar
            def _(act):
                for s in range(1, SLICES, 2):
                    if CUTS[s + 1] == NT:
                        act.wait_ge(x_zero, 1)
                    load_x(act, s)
                with nc.allow_non_contiguous_dma(reason="one dst of each chunk and each tile"):
                    act.dma_start(base_row[0:1, 0:FULL],
                                  row_set(dst, 0, FULL)[:, 0:1].rearrange("r o -> o r")).then_inc(base_in, 16)
                    act.dma_start(quad_first[:, :],
                                  dst[0:COUNTED * CHUNK].rearrange("(q t e) -> q t e", t=QT, e=P)[:, :, 0]
                                  ).then_inc(base_in, 16)
                act.dma_start(base_row[0:1, FULL:CHUNKS],
                              dst[E - CHUNK:E - CHUNK + 1].rearrange("(o r) -> o r", o=1)).then_inc(base_in, 16)
                for s in range(SLICES):
                    act.wait_ge(mean_sub, s + 1)
                    nc.scalar.activation(sq_sb[:, CUTS[s]:CUTS[s + 1], :], h_sb[:, CUTS[s]:CUTS[s + 1], :],
                                         ACT.Square).then_inc(squared, 1)
                act.wait_ge(var_made, SLICES)
                nc.scalar.activation(std[:, :], var[:, :], ACT.Sqrt, bias=eps_col[:, 0:1],
                                     scale=1.0 / F).then_inc(std_made, 1)
                act.wait_ge(h_made, SLICES)
                nc.scalar.copy(h_parts[:, :, 0, :], h_sb[:, :, :]).then_inc(part_made, 1)
                act.dma_start(w1_sb[0:F, :], w1[:, :]).then_inc(w_in, 16)
                act.dma_start(w1_sb[F:2 * F, :], w1[:, :]).then_inc(w_in, 16)
                act.dma_start(w2_sb[:, :], w2[:, :]).then_inc(w_in, 16)
                act.dma_start(b1_col[:, :], b1[:].rearrange("(p o) -> p o", o=1)).then_inc(w_in, 16)
                act.dma_start(b2_all[:, :], b2[:].rearrange("(o f) -> o f", o=1).to_broadcast([P, F])).then_inc(w_in, 16)
                def copy_rest(part):
                    act.wait_ge(rest_made, part)
                    nc.scalar.copy(h_parts[:, :, part, :], sq_sb).then_inc(part_made, 1)

                copy_rest(1)

                act.wait_ge(turned_used, JOB_ENDS[1])
                act.wait_ge(h_out, 16 * SLICES)

                def copy_parts():
                    nc.scalar.copy(parts_sb[:, :, :].rearrange("p q f -> p (q f)"),
                                   part_ps[:, 0:QG * 3 * F]).then_inc(parts_copied, 1)

                def group(g, b, i):
                    places = counts[b][:, 0:NT * CT * SPAN].rearrange("p (s t w) -> p s t w", s=NT, w=SPAN)
                    wait(act, parts_done, g - 1)
                    if not isinstance(g, int) or g >= 2:
                        copy_parts()
                    if isinstance(g, int) and g == 1 and pool_rows:
                        act.wait_ge(rows_measured, 3)
                    for u in range(PAIRS):
                        act.wait_ge(counted, g * PAIRS + (u + 1))
                        nc.scalar.copy(places[:, :, 2 * u:2 * u + 2, :].rearrange("p s t w -> p t s w"),
                                       count_ps[u % 2][:, :, 0:CODES].rearrange("p t (s w) -> p t s w", w=SPAN)
                                       ).then_inc(copied, 1)
                        if isinstance(g, int) and g == 0 and u == 8:
                            copy_rest(2)
                    if isinstance(g, int) and g == 1:
                        act.wait_ge(turned_used, JOBS)
                        act.dma_start(x_sb[:, 0:NT - 1, :], x_tiles(x)).then_inc(x_again, 16)
                        act.dma_start(x_sb[0:NLAST, NT - 1, :], x[(NT - 1) * P:N, :]).then_inc(x_again, 16)

                all_groups(act, group)
                for g in (GROUPS - 2, GROUPS - 1):
                    act.wait_ge(parts_done, g + 1)
                    act.wait_ge(placed, g)
                    copy_parts()

            @block.gpsimd
            def _(pool):
                nc.gpsimd.memset(ones[:, :], 1.0).then_inc(const_made, 1)
                pool.wait_ge(const_made, 1)
                nc.gpsimd.affine_select(out=ident[:, :], in_=ones[:, :], compare_op=ALU.is_equal, fill=0.0, base=0,
                                        pattern=[[-1, P]], channel_multiplier=1).then_inc(const_made, 1)
                nc.gpsimd.iota(iota_w[:, :], [[1, WINDOW]], base=0, channel_multiplier=0,
                               allow_small_or_imprecise_dtypes=True).then_inc(const_made, 1)
                nc.gpsimd.iota(iota_p[:, :], [[1, P]], base=0, channel_multiplier=0,
                               allow_small_or_imprecise_dtypes=True).then_inc(const_made, 1)
                nc.gpsimd.iota(iota_c[:, :], [[1, CODES]], base=0, channel_multiplier=0,
                               allow_small_or_imprecise_dtypes=True).then_inc(const_made, 1)
                nc.gpsimd.memset(agg[:, :], 0.0).then_inc(sums_added, 1)

                steps = [0]

                def pool_chain(instruction):
                    steps[0] += 1
                    instruction.then_inc(pool_done, 1)
                    pool.wait_ge(pool_done, steps[0])

                src_flat = src_col[:, :, :].rearrange("p c k -> p (c k)")

                def gather(g, b, i, tiles):
                    if isinstance(g, int):
                        pool.wait_ge(msg_in[b], 16 * sum(msg_dmas[b:g + 1:2]))
                    else:
                        pool.wait_ge(msg_in[b], i * 16 + 16)
                        pool.sem_inc(gather_turn, 1)
                    nc.gpsimd.tensor_copy(idx[b][:, 0:tiles], src_flat[:, bass.ds(gathered_first(g, b, i) * K, tiles)]).then_inc(idx_made, 1)
                    pool.wait_ge(idx_made, g + 1)
                    if not isinstance(g, int):
                        pool.sem_inc(gather_turn, 1)
                    for t in range(tiles):
                        nc.gpsimd.indirect_dma_start(
                            out=msg[b][:, t, :], out_offset=None, in_=h_dram[:, :],
                            in_offset=bass.IndirectOffsetOnAxis(ap=idx[b][:, t:t + 1], axis=0),
                            compute_op=ALU.add).then_inc(gathered[b], 16)

                def group(g, b, i):
                    if not gathered_chunks(g, b):
                        return
                    wait(pool, msgs_done, g - 1)
                    if not isinstance(g, int):
                        pool.sem_inc(gather_turn, 1)
                    gather(g, b, i, gathered_chunks(g, b) * K)

                def rest_of_h(part):
                    whole = h_sb[:, :, :] if part == 0 else sq_sb
                    pool.wait_ge(part_made, part + 1)
                    if part:
                        pool.wait_ge(rest_made, part)
                    nc.gpsimd.tensor_tensor(sq_sb, whole, h_parts[:, :, part, :], ALU.subtract).then_inc(rest_made, 1)

                if pool_rows:
                    rows_of(pool, nc.gpsimd, pool_chain, 2)
                rest_of_h(0)
                rest_of_h(1)
                pool.wait_ge(turned_used, JOB_ENDS[0])
                pool.wait_ge(h_out, 16 * SLICES)
                all_groups(pool, group)

            @block.vector
            def _(dve):
                steps = [0]

                def chain(instruction):
                    steps[0] += 1
                    instruction.then_inc(dve_done, 1)
                    dve.wait_ge(dve_done, steps[0])

                def measure(n):
                    rows, is_counted = ROWSETS[n][1:]
                    a, second = row_buffers(n)[4:6]
                    dve.wait_ge(rows_ready[n], 1)
                    for column, values in ((0, a), (2, second)) if is_counted else ((0, a),):
                        nc.vector.tensor_reduce(outside[0:rows, n, column:column + 1], values, AX.X, ALU.max)
                        last = nc.vector.tensor_reduce(outside[0:rows, n, column + 1:column + 2], values, AX.X, ALU.min)
                    last.then_inc(rows_measured, 1)

                def columns_of(n):
                    first, rows, is_counted = ROWSETS[n]
                    at = first if is_counted else first - COUNTED
                    dests = [rel_col[:, first:first + rows, :]] + (
                        [count_col[:, part, at * K:(at + rows) * K].rearrange("p (r k) -> p r k", k=K) for part in range(2)]
                        if is_counted else [src_col[:, at:at + rows, :]])
                    for j, dest in enumerate(dests, JOB_ENDS[n] - len(dests)):
                        dve.wait_ge(turned, j + 1)
                        nc.vector.tensor_copy(
                            dest.rearrange("p r k -> p k r"),
                            turn_ps[TURN_BANK[j]][:, 0:K * P].rearrange("p (k r) -> p k r", k=K)[:, :, 0:rows]
                        ).then_inc(turned_used, 1)
                    if first + rows == CHUNKS:
                        dve.wait_ge(turned_used, JOB_ENDS[n])
                        whole, rest = divmod(TWICE, K)
                        for lo, hi, used in ((0, rest, whole + 1), (rest, K, whole)):
                            if lo < hi and used:
                                twice = rel_col[0:used, CHUNKS - 1, lo:hi]
                                chain(nc.vector.tensor_scalar(twice, twice, FAR, None, ALU.add))

                def per_node(ap, s):
                    count = CUTS[s + 1] - CUTS[s]
                    return ap[:, CUTS[s]:CUTS[s + 1]].rearrange("p (t o) -> p t o", o=1).to_broadcast([P, count, F])

                def subtract_mean(s):
                    at = slice(CUTS[s], CUTS[s + 1])
                    dve.wait_ge(x_in[s], 16 * ((CUTS[s] < NT - 1) + (CUTS[s + 1] == NT)))
                    chain(nc.vector.tensor_reduce(mean[:, at], x_sb[:, at, :], AX.X, ALU.add))
                    chain(nc.vector.tensor_scalar(mean[:, at], mean[:, at], 1.0 / F, None, ALU.mult))
                    nc.vector.tensor_tensor(h_sb[:, at, :], x_sb[:, at, :], per_node(mean, s),
                                            ALU.subtract).then_inc(mean_sub, 1)

                def variance(s):
                    at = slice(CUTS[s], CUTS[s + 1])
                    dve.wait_ge(squared, s + 1)
                    nc.vector.tensor_reduce(var[:, at], sq_sb[:, at, :], AX.X, ALU.add).then_inc(var_made, 1)

                nc.vector.memset(x_sb[:, NT - 1, :], 0.0).then_inc(x_zero, 1)
                nc.vector.memset(eps_col[:, :], EPS)
                nc.vector.memset(outside[:, :, :], 0.0).then_inc(outside_cleared, 1)
                dve.wait_ge(outside_cleared, 1)
                rows_of(dve, nc.vector, chain, 0)
                measure(0)
                subtract_mean(0)
                columns_of(0)
                for s in range(1, SLICES):
                    subtract_mean(s)
                    variance(s - 1)
                if pool_rows:
                    dve.wait_ge(rows_in[2], 16 * rows_dmas[2])
                    split_src(2).then_inc(src_split, 1)
                variance(SLICES - 1)
                dve.wait_ge(std_made, 1)
                chain(nc.vector.reciprocal(rstd[:, :], std[:, :]))
                for s in range(SLICES):
                    part = h_sb[:, CUTS[s]:CUTS[s + 1], :]
                    nc.vector.scalar_tensor_tensor(out=part, in0=part, scalar=0.0, in1=per_node(rstd, s),
                                                   op0=ALU.max, op1=ALU.mult).then_inc(h_made, 1)

                rows_of(dve, nc.vector, chain, 1)
                measure(1)
                columns_of(1)
                nc.vector.memset(count_col[:, :, COUNTED * K:], 0.0)
                chain(nc.vector.memset(rel_col[:, CHUNKS:, :], 0.0))

                def quad_places():
                    dve.wait_ge(base_in, 48)
                    nc.vector.tensor_copy(quad_row[0:1, :], base_row[0:1, 0:COUNTED:QUAD])
                    chain(nc.vector.tensor_copy(quad_rel[:, :], quad_first[:, :]))
                    chain(nc.vector.tensor_scalar(quad_rel[:, :], quad_rel[:, :], quad_rel[:, 0:1], None, ALU.subtract))
                    nc.vector.tensor_reduce(outside[0:QUADS, len(ROWSETS), 0:1], quad_rel[:, :], AX.X, ALU.max)
                    nc.vector.tensor_reduce(outside[0:QUADS, len(ROWSETS), 1:2], quad_rel[:, :], AX.X, ALU.min)
                    nc.vector.tensor_tensor(
                        quad_rows[:, :, :],
                        quad_rel[:, :].rearrange("q (t o) -> q t o", o=1).to_broadcast([QUADS, QT, SPAN]),
                        iota_w[0:QUADS, 0:SPAN].rearrange("q (o d) -> q o d", o=1).to_broadcast([QUADS, QT, SPAN]),
                        ALU.add).then_inc(quads_ready, 1)
                    dve.wait_ge(quads_ready, 1)

                def quad_columns():
                    dve.wait_ge(turned, JOBS)
                    nc.vector.tensor_copy(place_col[:, :], turn_ps[TURN_BANK[JOBS - 1]][:, 0:QUADS]).then_inc(turned_used, 1)

                def how_far():
                    dve.wait_ge(rows_measured, len(ROWSETS))
                    for n, column, least in ((slice(0, len(ROWSETS)), 0, 1 - WINDOW), (slice(0, len(ROWSETS)), 2, 1 - SPAN),
                                             (slice(len(ROWSETS), len(ROWSETS) + 1), 0, SPAN - QSPAN)):
                        nc.vector.tensor_scalar(outside[:, n, column], outside[:, n, column], float(least), None, ALU.add)
                        last = nc.vector.tensor_scalar(outside[:, n, column + 1], outside[:, n, column + 1], -1.0, None,
                                                       ALU.mult)
                    chain(last)
                    nc.vector.tensor_reduce(worst[:, :], outside[:, :, :], AX.XY, ALU.max).then_inc(worst_made, 1)

                def make_flag():
                    dve.wait_ge(worst_turned, 1)
                    chain(nc.vector.tensor_reduce(flag_f[:, :], placed_ps[0:1, 0:P], AX.X, ALU.max))
                    chain(nc.vector.tensor_scalar(flag_f[:, :], flag_f[:, :], 0.0, 1.0, ALU.max, ALU.min))
                    nc.vector.tensor_copy(flag_i[:, :], flag_f[:, :]).then_inc(flag_made, 1)

                def rest_of_preparation(g, t):
                    if g == 0:
                        if t == 2 * TURN_AT[2] + 1 and pool_rows:
                            columns_of(2)
                        if t == 11 and LATER:
                            rows_of(dve, nc.vector, chain, 3)
                        if t == 24 and pool_rows:
                            measure(2)
                        if t == 2 * TURN_AT[3] + 1 and LATER:
                            columns_of(3)
                    else:
                        if t == 6 and LATER:
                            measure(3)
                        if t == 17:
                            quad_places()
                            how_far()
                        if t == 2 * QUADS_AT + 1:
                            quad_columns()
                        if t == 2 * WORST_AT + 1:
                            make_flag()
                            dve.wait_ge(turned_used, JOBS)

                rel_flat = rel_col[:, :, :].rearrange("p c k -> p (c k)")

                def windows(out_ap, at, tiles):
                    return nc.vector.tensor_tensor(
                        out_ap, iota_w[:, :].rearrange("p (o w) -> p o w", o=1).to_broadcast([P, tiles, WINDOW]),
                        rel_flat[:, bass.ds(at, tiles)].rearrange("p (t o) -> p t o", o=1)
                        .to_broadcast([P, tiles, WINDOW]), ALU.is_equal)

                def gathered_windows(g, b, i):
                    tiles = gathered_chunks(g, b) * K
                    windows(m_hot[b][:, 0:tiles, :], gathered_first(g, b, i) * K + COUNTED * K, tiles
                            ).then_inc(m_hots_made, 1)

                def take_columns(b, g):
                    nc.vector.tensor_copy(group_code[b][:, :], count_col[:, 0, bass.ds(g * CT, CT)])
                    nc.vector.tensor_copy(group_lo[b][:, :], count_col[:, 1, bass.ds(g * CT, CT)]
                                          ).then_inc(columns_taken, 1)

                def load_bases(row, first, count):
                    _, bases = nc.values_load_multi_w_load_instructions(
                        row[0:1, bass.ds(first, count)], engines=[mybir.EngineType.DVE],
                        min_val=0, max_val=N - 1, skip_runtime_bounds_check_because="dst is a node number")
                    return bases

                def add_window(base, sums, done):
                    half, width = sums.shape
                    window = agg[0:half, bass.ds(base, width)]
                    dve.wait_ge(sums_added, done)
                    nc.vector.tensor_tensor(window, window, sums, ALU.add).then_inc(sums_added, 1)

                def chunk_sums(bank, half, c):
                    return bank[0:half, c * WINDOW:(c + 1) * WINDOW]

                def quad_sums(q):
                    return placed_ps[:, q * QSPAN:(q + 1) * QSPAN]

                def places(g):
                    nc.vector.tensor_tensor(
                        place_hot[:, :, :], iota_p[:, :].rearrange("p (o w) -> p o w", o=1).to_broadcast([P, QG, QSPAN]),
                        place_col[:, bass.ds(g * QG, QG)].rearrange("p (q o) -> p q o", o=1)
                        .to_broadcast([P, QG, QSPAN]), ALU.is_equal).then_inc(place_made, 1)

                def group(g, b, i):
                    behind = 2 if not isinstance(g, int) else g
                    done = done_before(g, b, i)
                    if behind >= 2:
                        places(g - 2)
                    windows(e_hot[b][:, :, :], g * CT, CT)
                    dve.wait_ge(columns_taken, g + 1)
                    for t in range(CT):
                        u = t // 2
                        if t % 2 == 0:
                            wait(dve, counted, g * PAIRS + (u - SLOTS + 1))
                        if t % LB == 0:
                            nc.vector.tensor_tensor(
                                lo_hot[t // LB % 2][:, :, :], iota_b[:, :, :],
                                group_lo[b][:, t:t + LB].rearrange("p (o t) -> p o t", o=1).to_broadcast([P, P, LB]),
                                ALU.is_equal)
                        made = nc.vector.tensor_scalar(code_hot[u % SLOTS][:, t % 2, :], iota_c[:, :],
                                                       group_code[b][:, t:t + 1], None, ALU.is_equal)
                        if t % 2 == 1:
                            made.then_inc(hots_made, 1)

                        if EDGE_AT <= t < EDGE_AT + CG and behind >= 1:
                            if t == EDGE_AT:
                                dve.wait_ge(edges_done, g)
                                edge_bases = load_bases(base_row, (g - 1) * CG, CG)
                            c = t - EDGE_AT
                            add_window(edge_bases[c], chunk_sums(edge_ps, F, c), done + c)
                        chunks = gathered_chunks(g - 1, 1 - b)
                        if MSG_AT <= t < MSG_AT + chunks:
                            if t == MSG_AT:
                                dve.wait_ge(msgs_done, g)
                                msg_bases = load_bases(base_row, gathered_first(g - 1, 1 - b, i if b else i - 1) + COUNTED, chunks)
                            c = t - MSG_AT
                            add_window(msg_bases[c], chunk_sums(msg_ps, F, c), done + CG + c)
                        if PLACE_AT <= t < PLACE_AT + QG and behind >= 2:
                            if t == PLACE_AT:
                                dve.wait_ge(placed, g - 1)
                                quad_bases = load_bases(quad_row, (g - 2) * QG, QG)
                            q = t - PLACE_AT
                            add_window(quad_bases[q], quad_sums(q), done + (CG + chunks) + q)
                        if t == PLACE_AT + QG and gathered_chunks(g + 1, 1 - b):
                            gathered_windows(g + 1, 1 - b, i + b)
                        if t == CT - 1:
                            take_columns(1 - b, g + 1)
                        if isinstance(g, int) and g < 2:
                            rest_of_preparation(g, t)

                dve.wait_ge(const_made, 5)
                dve.wait_ge(base_in, 48)
                nc.vector.tensor_copy(iota_b[:, :, :], iota_p[:, :].rearrange("p (w o) -> p w o", o=1)
                                      .to_broadcast([P, P, LB])).then_inc(iota_made, 1)
                dve.wait_ge(iota_made, 1)
                dve.wait_ge(turned_used, JOB_ENDS[1])
                gathered_windows(0, 0, 0)
                take_columns(0, 0)
                all_groups(dve, group)
                places(GROUPS - 2)
                done = done_before(GROUPS)
                dve.wait_ge(edges_done, GROUPS)
                bases = load_bases(base_row, COUNTED - CG, CG)
                for c in range(CG):
                    add_window(bases[c], chunk_sums(edge_ps, F, c), done + c)
                done += CG
                chunks = gathered_chunks(GROUPS - 1, (GROUPS - 1) % 2)
                if chunks:
                    dve.wait_ge(msgs_done, GROUPS)
                    bases = load_bases(base_row, GATHERED[GROUPS - 1][0], chunks)
                    for c in range(chunks):
                        add_window(bases[c], chunk_sums(msg_ps, F, c), done + c)
                done += chunks
                for g in (GROUPS - 2, GROUPS - 1):
                    dve.wait_ge(placed, g + 1)
                    if g < GROUPS - 1:
                        places(g + 1)
                    bases = load_bases(quad_row, g * QG, QG)
                    for q in range(QG):
                        add_window(bases[q], quad_sums(q), done + q)
                    done += QG
                    if g < GROUPS - 1:
                        dve.wait_ge(w_in, 80)
                        dve.wait_ge(x_again, 32)
                        nc.vector.tensor_tensor(x_sb[:, :, :], x_sb[:, :, :],
                                                b2_all[:, :].rearrange("p (o f) -> p o f", o=1).to_broadcast([P, NT, F]),
                                                ALU.add).then_inc(bias_added, 1)

            @block.tensor
            def _(pe):
                pe.wait_ge(const_made, 2)

                def turn(n):
                    rows, is_counted = ROWSETS[n][1:]
                    code, _, a, second, third = row_buffers(n)[2:]
                    pe.wait_ge(rows_ready[n], 1)
                    sources = [(a, True)] + ([(code, False), (third, False)] if is_counted else [(second, True)])
                    for j, (source, strided) in enumerate(sources, JOB_ENDS[n] - len(sources)):
                        wait(pe, turned_used, turn_free(j))
                        for k in range(K):
                            part = source[:, k:CHUNK:K] if strided else source[:, k * P:(k + 1) * P]
                            last = nc.tensor.transpose(turn_ps[TURN_BANK[j]][:, k * P:k * P + rows], part,
                                                       ident[0:rows, 0:rows])
                        last.then_inc(turned, 1)

                def rest_of_preparation(g, u):
                    if g == 0:
                        if u == TURN_AT[2] and pool_rows:
                            turn(2)
                        if u == TURN_AT[3] and LATER:
                            turn(3)
                    else:
                        if u == QUADS_AT:
                            pe.wait_ge(quads_ready, 1)
                            wait(pe, turned_used, turn_free(JOBS - 1))
                            nc.tensor.transpose(turn_ps[TURN_BANK[JOBS - 1]][:, 0:QUADS],
                                                quad_rows[:, :, :].rearrange("q t d -> q (t d)"),
                                                ident[0:QUADS, 0:QUADS]).then_inc(turned, 1)
                        if u == WORST_AT:
                            pe.wait_ge(worst_made, 1)
                            pe.wait_ge(turned_used, JOBS)
                            nc.tensor.transpose(placed_ps[0:1, 0:P], worst[:, 0:1], ident[:, :]).then_inc(worst_turned, 1)

                def counts_times_h(b, his):
                    stacked = counts[b][:, 0:NT * CT * SPAN].rearrange("p (s q c) -> p s q c", s=NT, q=QG)
                    for s in his:
                        for q in range(QG):
                            last = nc.tensor.matmul(part_ps[:, q * 3 * F:(q + 1) * 3 * F], stacked[:, s, q, :],
                                                    h_parts[:, s, :, :].rearrange("p a f -> p (a f)"),
                                                    start=(s == 0 and q == 0), stop=(s == NT - 1),
                                                    skip_group_check=True)
                        if s == NT - 1:
                            last.then_inc(parts_done, 1)

                def place():
                    for q in range(QG):
                        at = slice(q * QSPAN, (q + 1) * QSPAN)
                        half = F * (q % 2)
                        nc.tensor.matmul(placed_ps[:, at], parts_sb[:, q, 0:2 * F], place_hot[:, q, :],
                                         start=True, stop=False, skip_group_check=True)
                        last = nc.tensor.matmul(placed_ps[half:half + F, at], parts_sb[:, q, 2 * F:3 * F],
                                                place_hot[:, q, :], start=False, stop=True, skip_group_check=True)
                    last.then_inc(placed, 1)

                def gathered_products(b, chunks):
                    for c in range(chunks):
                        for t in range(c * K, (c + 1) * K):
                            last = nc.tensor.matmul(msg_ps[0:F, c * WINDOW:(c + 1) * WINDOW], msg[b][:, t, :],
                                                    m_hot[b][:, t, :], start=(t % K == 0), stop=(t % K == K - 1))
                    last.then_inc(msgs_done, 1)

                def group(g, b, i):
                    known = isinstance(g, int)
                    for u in range(PAIRS):
                        pe.wait_ge(hots_made, g * PAIRS + (u + 1))
                        wait(pe, copied, g * PAIRS + (u - 1))
                        for j in range(2):
                            last = nc.tensor.matmul(count_ps[u % 2][:, j, 0:CODES],
                                                    lo_hot[2 * u // LB % 2][:, :, (2 * u + j) % LB],
                                                    code_hot[u % SLOTS][:, j, :], start=True, stop=True)
                        last.then_inc(counted, 1)
                        if known and g < 2:
                            rest_of_preparation(g, u)
                        if u == EDGE_FROM:
                            if known:
                                pe.wait_ge(edges_in[b], 16 * (g // 2 + 1))
                            else:
                                pe.wait_ge(edges_in[b], i * 16 + 16)
                        for t in share(CT, EDGE_FROM, PAIRS - 1, u):
                            last = nc.tensor.matmul(edge_ps[0:F, t // K * WINDOW:(t // K + 1) * WINDOW],
                                                    edges[b][:, t, :], e_hot[b][:, t, :],
                                                    start=(t % K == 0), stop=(t % K == K - 1))
                            if t == CT - 1:
                                last.then_inc(edges_done, 1)
                        if u == 0 and not (known and g < 1):
                            pe.wait_ge(copied, g * PAIRS)
                            if known and g == 1:
                                pe.wait_ge(part_made, 3)
                                pe.wait_ge(turned_used, JOB_ENDS[-1])
                            if not (known and g < 2):
                                pe.wait_ge(parts_copied, g - 1)
                        if not (known and g < 1):
                            counts_times_h(1 - b, share(NT, 0, PAIRS - 1, u))
                        if u == 1 and not (known and g < 2):
                            pe.wait_ge(place_made, g - 1)
                            place()
                    chunks = gathered_chunks(g, b)
                    if not chunks:
                        return
                    if known:
                        pe.wait_ge(gathered[b], 16 * K * sum(gathered_chunks(n, b) for n in range(b, g + 1, 2)))
                    else:
                        pe.wait_ge(gathered[b], i * (16 * K * GGS[b]) + 16 * K * GGS[b])
                    pe.wait_ge(m_hots_made, g + 1)
                    gathered_products(b, chunks)

                turn(0)
                turn(1)
                all_groups(pe, group)
                pe.wait_ge(copied, GROUPS * PAIRS)
                pe.wait_ge(parts_copied, GROUPS - 1)
                pe.wait_ge(place_made, GROUPS - 1)
                place()
                counts_times_h((GROUPS - 1) % 2, range(NT))
                pe.wait_ge(parts_copied, GROUPS)
                pe.wait_ge(place_made, GROUPS)
                pe.wait_ge(sums_added, done_before(GROUPS + 1))
                place()

        anew = nc.values_load(flag_i[0:1, 0:1], min_val=0, max_val=1,
                              skip_runtime_bounds_check_because="made as 0 or 1")
        g_split, g_rows, g_cleared, g_in, g_read, g_gath, g_hots, g_sums, g_adds, g_cols, g_idx = [
            sem(s) for s in ("g_split", "g_rows", "g_cleared", "g_in", "g_read", "g_gathered", "g_hot_made", "g_summed", "g_added",
                             "g_col_made", "g_idx_used")]
        G_TILES = E // P
        G_TWICE = (G_TILES + 1) * P - E
        with nc.If(anew):
            with nc.Block() as block:

                @block.sync
                def _(sp):
                    def load(lo, n):
                        sp.wait_ge(g_adds, n * NT + 1)
                        sp.dma_start(g_dst[:, :], col(dst, lo)).then_inc(g_in, 16)
                        sp.dma_start(g_src[:, :], col(src, lo)).then_inc(g_in, 16)

                    with sp.Fori(0, G_TILES) as i:
                        load(i * P, i)
                    load(E - P, G_TILES)

                @block.scalar
                def _(act):
                    def load(lo, n):
                        act.wait_ge(g_adds, n * NT + 1)
                        act.dma_start(g_msg[:, 0, :], edge[bass.ds(lo, P), :]).then_inc(g_in, 16)

                    with act.Fori(0, G_TILES) as i:
                        load(i * P, i)
                    load(E - P, G_TILES)

                @block.gpsimd
                def _(pool):
                    def gather(n):
                        pool.wait_ge(g_rows, n + 1)
                        pool.sem_inc(gather_turn, 1)
                        nc.gpsimd.indirect_dma_start(
                            out=g_msg[:, 1, :], out_offset=None, in_=h_dram[:, :],
                            in_offset=bass.IndirectOffsetOnAxis(ap=g_row[:, 0:1], axis=0)).then_inc(g_gath, 16)

                    with pool.Fori(0, G_TILES) as i:
                        gather(i)
                    gather(G_TILES)

                @block.vector
                def _(dve):
                    def tile(n):
                        dve.wait_ge(g_in, n * 48 + 48)
                        nc.vector.tensor_scalar(g_hi[:, :], g_src[:, :], P.bit_length() - 1, None, ALU.logical_shift_right)
                        nc.vector.tensor_scalar(g_src[:, :], g_src[:, :], P - 1, None, ALU.bitwise_and).then_inc(g_split, 1)
                        dve.wait_ge(g_split, n + 1)
                        nc.vector.scalar_tensor_tensor(out=g_row[:, :], in0=g_src[:, :], scalar=float(NT), in1=g_hi[:, :],
                                                       op0=ALU.mult, op1=ALU.add).then_inc(g_rows, 1)
                        nc.vector.tensor_copy(g_rel[:, :], g_dst[:, :]).then_inc(g_cols, 1)

                    def windows(n):
                        with dve.Fori(0, NT) as w:
                            done = dve.snap(n * NT + w)
                            dve.wait_ge(g_cols, n * (NT + 1) + w + 1)
                            nc.vector.tensor_scalar(g_hot[:, :], iota_p[:, :], g_rel[:, 0:1], None,
                                                    ALU.is_equal).then_inc(g_hots, 1)
                            nc.vector.tensor_scalar(g_rel[:, :], g_rel[:, :], float(-P), None, ALU.add).then_inc(g_cols, 1)
                            dve.wait_ge(g_sums, done + 1)
                            part = agg[0:F, bass.ds(w * P, P)]
                            nc.vector.tensor_tensor(part, part, sum_ps[0][0:F, 0:P], ALU.add).then_inc(g_adds, 1)

                    nc.vector.memset(g_far[:, :], 0.0).then_inc(g_cleared, 1)
                    dve.wait_ge(g_cleared, 1)
                    nc.vector.memset(g_far[0:G_TWICE, :], FAR).then_inc(g_cleared, 1)
                    nc.vector.memset(agg[:, :], 0.0).then_inc(g_adds, 1)
                    dve.wait_ge(g_cleared, 2)
                    dve.wait_ge(g_adds, 1)
                    with dve.Fori(0, G_TILES) as i:
                        tile(i)
                        windows(i)
                    tile(G_TILES)
                    dve.wait_ge(g_cols, G_TILES * (NT + 1) + 1)
                    nc.vector.tensor_tensor(g_rel[:, :], g_rel[:, :], g_far[:, :], ALU.add).then_inc(g_read, 1)
                    dve.wait_ge(g_read, 1)
                    windows(G_TILES)

                @block.tensor
                def _(pe):
                    def tile(n):
                        with pe.Fori(0, NT) as w:
                            pe.wait_ge(g_gath, n * 16 + 16)
                            pe.wait_ge(g_hots, n * NT + w + 1)
                            nc.tensor.matmul(sum_ps[0][0:F, 0:P], g_msg[:, 0, :], g_hot[:, :], start=True, stop=False)
                            nc.tensor.matmul(sum_ps[0][0:F, 0:P], g_msg[:, 1, :], g_hot[:, :],
                                             start=False, stop=True).then_inc(g_sums, 1)

                    with pe.Fori(0, G_TILES) as i:
                        tile(i)
                    tile(G_TILES)

        hid_made, relu_made, rows_made, rows_added, rows_out = [
            sem(s) for s in ("hid_made", "relu_made", "rows_made", "rows_added", "rows_out")]
        with nc.Block() as block:
            BT = BLK // P

            def tiles_of(n):
                lo, count = BLOCKS[n]
                return [(t, min(P, lo + count - t)) for t in range(lo, lo + count, P)]

            @block.tensor
            def _(pe):
                def hidden(n):
                    lo, count = BLOCKS[n]
                    if n >= 2:
                        pe.wait_ge(relu_made, n - 1)
                    nc.tensor.matmul(hid_ps[n % 2][:, 0:count], w1_sb[:, :], agg[:, lo:lo + count],
                                     start=True, stop=True).then_inc(hid_made, 1)

                pe.wait_ge(w_in, 80)
                hidden(0)
                for n in range(len(BLOCKS)):
                    if n + 1 < len(BLOCKS):
                        hidden(n + 1)
                    pe.wait_ge(relu_made, n + 1)
                    if n >= 2:
                        pe.wait_ge(rows_added, n - 1)
                    for j, (lo, count) in enumerate(tiles_of(n)):
                        last = nc.tensor.matmul(out_ps[n % 2][0:count, j * F:(j + 1) * F],
                                                hid_sb[n % 2][:, j * P:j * P + count], w2_sb[:, :],
                                                start=True, stop=True)
                    last.then_inc(rows_made, 1)

            @block.scalar
            def _(act):
                act.wait_ge(w_in, 80)
                for n, (lo, count) in enumerate(BLOCKS):
                    act.wait_ge(hid_made, n + 1)
                    if n >= 2:
                        act.wait_ge(rows_made, n - 1)
                    nc.scalar.activation(hid_sb[n % 2][:, 0:count], hid_ps[n % 2][:, 0:count], ACT.Relu,
                                         bias=b1_col[:, 0:1]).then_inc(relu_made, 1)

            @block.vector
            def _(dve):
                dve.wait_ge(bias_added, 1)
                for n in range(len(BLOCKS)):
                    dve.wait_ge(rows_made, n + 1)
                    parts = tiles_of(n)
                    whole = sum(count == P for _, count in parts)
                    t0 = n * BT
                    if whole:
                        last = nc.vector.tensor_tensor(
                            o_sb[:, t0:t0 + whole, :],
                            out_ps[n % 2][:, 0:whole * F].rearrange("p (t f) -> p t f", f=F),
                            x_sb[:, t0:t0 + whole, :], ALU.add)
                    if whole < len(parts):
                        count = parts[whole][1]
                        last = nc.vector.tensor_tensor(o_sb[0:count, t0 + whole, :],
                                                       out_ps[n % 2][0:count, whole * F:(whole + 1) * F],
                                                       x_sb[0:count, t0 + whole, :], ALU.add)
                    last.then_inc(rows_added, 1)

            @block.sync
            def _(sp):
                sent = 0
                for n in range(len(BLOCKS)):
                    sp.wait_ge(rows_added, n + 1)
                    parts = tiles_of(n)
                    whole = sum(count == P for _, count in parts)
                    t0 = n * BT
                    if whole:
                        sp.dma_start(out[t0 * P:(t0 + whole) * P, :].rearrange("(t p) f -> p t f", p=P),
                                     o_sb[:, t0:t0 + whole, :]).then_inc(rows_out, 16)
                        sent += 16
                    if whole < len(parts):
                        lo, count = parts[whole]
                        sp.dma_start(out[lo:lo + count, :], o_sb[0:count, t0 + whole, :]).then_inc(rows_out, 16)
                        sent += 16
                sp.wait_ge(rows_out, sent)


def kernel(**inputs):
    import concourse.bacc as bacc
    from concourse.bass_utils import run_bass_kernel_spmd

    nc = bacc.Bacc("TRN2", target_bir_lowering=False, num_devices=1)
    names = ["x", "src", "dst", "edge_attr_64", "L0_gnn_W1", "L0_gnn_b1", "L0_gnn_W2", "L0_gnn_b2"]
    arrays, args = {}, []
    for name in names:
        a = np.ascontiguousarray(inputs[name])
        arrays[f"in_{name}"] = a
        args.append(nc.dram_tensor(f"in_{name}", a.shape, mybir.dt.from_np(a.dtype), kind="ExternalInput").ap())
    args.append(nc.dram_tensor("out_0", inputs["x"].shape, mybir.dt.float32, kind="ExternalOutput").ap())
    build_gnn_layer(nc, *args)
    return run_bass_kernel_spmd(nc, [arrays], core_ids=[0]).results[0]["out_0"]
```
